# Optimizing a Trainium2 kernel written in Bass

```python
import numpy as np
import jax
import jax.numpy as jnp

def _softmax(x, axis=-1):
    return jax.nn.softmax(x, axis=axis)

def _gelu(x):
    return jax.nn.gelu(x, approximate=True)

def _silu(x):
    return jax.nn.silu(x)

def _sigmoid(x):
    return jax.nn.sigmoid(x)

def _layernorm(x, axis=-1, eps=1e-05):
    m = jnp.mean(x, axis=axis, keepdims=True)
    v = jnp.var(x, axis=axis, keepdims=True)
    return (x - m) / jnp.sqrt(v + eps)

def _scatter_add(tgt, idx, src, axis=0):
    return tgt.at[idx].add(src)

def _segment_sum(src, seg, n):
    return jax.ops.segment_sum(src, seg, n)
kernel_name = 'mk_macaron_d1_jaxref_r4_685585'

def setup_inputs(seed: int=0):
    np.random.seed(seed)
    _w = jnp.asarray

    def _L0_attn_setup():
        import jax, jax.numpy as jnp
        import numpy as np
        import math
        DIM = 256
        NUM_HEADS = 16
        HEAD_DIM = DIM // NUM_HEADS
        BATCH = 4
        SEQ = 1024

        def _feature_map(x, R):
            x = x / math.sqrt(HEAD_DIM)
            proj = jnp.einsum('bhnd,dm->bhnm', x, R)
            sq_norm = jnp.sum(x * x, axis=-1, keepdims=True)
            return jnp.exp(proj - 0.5 * sq_norm)
        key = jax.random.key(seed)
        ks = jax.random.split(key, 10)
        s = 1.0 / math.sqrt(DIM)
        return {'x': jax.random.normal(ks[0], (BATCH, SEQ, DIM), dtype=jnp.float32), 'Wq': jax.random.normal(ks[1], (DIM, DIM), dtype=jnp.float32) * s, 'bq': jax.random.normal(ks[2], (DIM,), dtype=jnp.float32) * 0.01, 'Wk': jax.random.normal(ks[3], (DIM, DIM), dtype=jnp.float32) * s, 'bk': jax.random.normal(ks[4], (DIM,), dtype=jnp.float32) * 0.01, 'Wv': jax.random.normal(ks[5], (DIM, DIM), dtype=jnp.float32) * s, 'bv': jax.random.normal(ks[6], (DIM,), dtype=jnp.float32) * 0.01, 'Wo': jax.random.normal(ks[7], (DIM, DIM), dtype=jnp.float32) * s, 'bo': jax.random.normal(ks[8], (DIM,), dtype=jnp.float32) * 0.01, 'R': jax.random.normal(ks[9], (HEAD_DIM, HEAD_DIM), dtype=jnp.float32) * 0.4}
    _L0_attn_in = _L0_attn_setup()

    def _L0_ffn_setup():
        import jax, jax.numpy as jnp
        import numpy as np
        B, S, M, E, DFF = (4, 512, 256, 8, 1024)
        CAPACITY_FACTOR = 1.25

        def _top1_gate(tokens, wg, capacity):
            gates = jax.nn.softmax(tokens @ wg)
            expert_idx = jnp.argmax(gates, axis=-1)
            mask1 = jax.nn.one_hot(expert_idx, gates.shape[-1], dtype=gates.dtype)
            pos = jnp.sum(jnp.cumsum(mask1, axis=0) * mask1, axis=-1).astype(jnp.int32) - 1
            keep = (pos < capacity).astype(gates.dtype)
            mask1c = mask1 * keep[:, None]
            gates1 = jnp.sum(gates * mask1c, axis=-1)
            loc_oh = jax.nn.one_hot(pos, capacity, dtype=gates.dtype)
            combine = gates1[:, None, None] * mask1c[:, :, None] * loc_oh[:, None, :]
            dispatch = (combine > 0).astype(tokens.dtype)
            return (combine, dispatch)
        key = jax.random.key(seed)
        k = jax.random.split(key, 5)
        x = jax.random.normal(k[0], (B, S, M), dtype=jnp.float32)
        wg = jax.random.normal(k[1], (M, E), dtype=jnp.float32) * 0.02
        w1 = jax.random.normal(k[2], (E, M, DFF), dtype=jnp.float32) * 0.02
        b1 = jnp.zeros((E, DFF), dtype=jnp.float32)
        w2 = jax.random.normal(k[3], (E, DFF, M), dtype=jnp.float32) * 0.02
        b2 = jnp.zeros((E, M), dtype=jnp.float32)
        return {'x': x, 'wg': wg, 'w1': w1, 'b1': b1, 'w2': w2, 'b2': b2}
    _L0_ffn_in = _L0_ffn_setup()
    _d = {'L0_attn_x': _L0_attn_in['x'], 'L0_attn_Wq': _L0_attn_in['Wq'], 'L0_attn_bq': _L0_attn_in['bq'], 'L0_attn_Wk': _L0_attn_in['Wk'], 'L0_attn_bk': _L0_attn_in['bk'], 'L0_attn_Wv': _L0_attn_in['Wv'], 'L0_attn_bv': _L0_attn_in['bv'], 'L0_attn_Wo': _L0_attn_in['Wo'], 'L0_attn_bo': _L0_attn_in['bo'], 'L0_attn_R': _L0_attn_in['R'], 'L0_ffn_wg': _L0_ffn_in['wg'], 'L0_ffn_w1': _L0_ffn_in['w1'], 'L0_ffn_b1': _L0_ffn_in['b1'], 'L0_ffn_w2': _L0_ffn_in['w2'], 'L0_ffn_b2': _L0_ffn_in['b2']}
    _x0 = _d['L0_attn_x']
    _d['L0_attn_x'] = jax.random.normal(jax.random.fold_in(jax.random.key(seed), 1), (8, 512, 256), dtype=_x0.dtype)
    del _x0
    return _d

def reference(L0_attn_x, L0_attn_Wq, L0_attn_bq, L0_attn_Wk, L0_attn_bk, L0_attn_Wv, L0_attn_bv, L0_attn_Wo, L0_attn_bo, L0_attn_R, L0_ffn_wg, L0_ffn_w1, L0_ffn_b1, L0_ffn_w2, L0_ffn_b2):

    def _L0_attn_ref(x, Wq, bq, Wk, bk, Wv, bv, Wo, bo, R):
        import jax, jax.numpy as jnp
        import numpy as np
        import math
        DIM = 256
        NUM_HEADS = 16
        HEAD_DIM = DIM // NUM_HEADS
        BATCH = 4
        SEQ = 1024

        def _feature_map(x, R):
            x = x / math.sqrt(HEAD_DIM)
            proj = jnp.einsum('bhnd,dm->bhnm', x, R)
            sq_norm = jnp.sum(x * x, axis=-1, keepdims=True)
            return jnp.exp(proj - 0.5 * sq_norm)
        b, n, _ = x.shape
        h, d = (NUM_HEADS, HEAD_DIM)

        def split_heads(t):
            return t.reshape(b, n, h, d).transpose(0, 2, 1, 3)
        q = split_heads(x @ Wq.T + bq)
        k = split_heads(x @ Wk.T + bk)
        v = split_heads(x @ Wv.T + bv)
        q_prime = _feature_map(q, R)
        k_prime = _feature_map(k, R)
        kv = jnp.einsum('bhnd,bhne->bhde', k_prime, v)
        z = 1.0 / (jnp.sum(q_prime, axis=-1) + 1e-08)
        out = jnp.einsum('bhnd,bhde,bhn->bhne', q_prime, kv, z)
        out = out.transpose(0, 2, 1, 3).reshape(b, n, DIM)
        return out @ Wo.T + bo

    def _L0_ffn_ref(x, wg, w1, b1, w2, b2):
        import jax, jax.numpy as jnp
        import numpy as np
        B, S, M, E, DFF = (4, 512, 256, 8, 1024)
        CAPACITY_FACTOR = 1.25

        def _top1_gate(tokens, wg, capacity):
            gates = jax.nn.softmax(tokens @ wg)
            expert_idx = jnp.argmax(gates, axis=-1)
            mask1 = jax.nn.one_hot(expert_idx, gates.shape[-1], dtype=gates.dtype)
            pos = jnp.sum(jnp.cumsum(mask1, axis=0) * mask1, axis=-1).astype(jnp.int32) - 1
            keep = (pos < capacity).astype(gates.dtype)
            mask1c = mask1 * keep[:, None]
            gates1 = jnp.sum(gates * mask1c, axis=-1)
            loc_oh = jax.nn.one_hot(pos, capacity, dtype=gates.dtype)
            combine = gates1[:, None, None] * mask1c[:, :, None] * loc_oh[:, None, :]
            dispatch = (combine > 0).astype(tokens.dtype)
            return (combine, dispatch)
        d_model = x.shape[-1]
        tokens = x.reshape(-1, d_model)
        T = tokens.shape[0]
        num_experts = wg.shape[1]
        capacity = int(CAPACITY_FACTOR * T / num_experts)
        combine, dispatch = _top1_gate(tokens, wg, capacity)
        dispatched = jnp.einsum('sec,sm->ecm', dispatch, tokens)
        h = jax.nn.relu(jnp.einsum('ecm,emf->ecf', dispatched, w1) + b1[:, None, :])
        expert_out = jnp.einsum('ecf,efm->ecm', h, w2) + b2[:, None, :]
        combined = jnp.einsum('sec,ecm->sm', combine, expert_out)
        return combined.reshape(x.shape)
    x = L0_attn_x
    x = x + 0.5 * _L0_ffn_ref(_layernorm(x, axis=-1), L0_ffn_wg, L0_ffn_w1, L0_ffn_b1, L0_ffn_w2, L0_ffn_b2)
    x = x + _L0_attn_ref(_layernorm(x, axis=-1), L0_attn_Wq, L0_attn_bq, L0_attn_Wk, L0_attn_bk, L0_attn_Wv, L0_attn_bv, L0_attn_Wo, L0_attn_bo, L0_attn_R)
    x = x + 0.5 * _L0_ffn_ref(_layernorm(x, axis=-1), L0_ffn_wg, L0_ffn_w1, L0_ffn_b1, L0_ffn_w2, L0_ffn_b2)
    return x

_drawn_inputs = setup_inputs


def setup_inputs(seed=0):
    import zlib

    import numpy as np

    out = dict(_drawn_inputs(seed))
    spreads = {'L0_ffn_b1': (0.0, 0.331), 'L0_ffn_b2': (0.0, 0.1)}
    factors = {'L0_attn_bq': 63.758,
     'L0_attn_bk': 8.0,
     'L0_attn_bo': 64.0,
     'L0_ffn_wg': 2.972,
     'L0_ffn_w1': 4.046}
    for name, (base, spread) in spreads.items():
        noise = np.random.default_rng([zlib.crc32(name.encode()), seed]).standard_normal(out[name].shape)
        drawn = base * np.exp(spread * noise) if base else spread * noise
        out[name] = jnp.asarray(drawn.astype(out[name].dtype))
    for name, factor in factors.items():
        out[name] = (out[name] * factor).astype(out[name].dtype)
    return out
```

```python
from contextlib import ExitStack

import concourse.bass as bass
from concourse import mybir

F32 = mybir.dt.float32
I32 = mybir.dt.int32
ALU = mybir.AluOpType
ACT = mybir.ActivationFunctionType
AX = mybir.AxisListType

P = 128
HEAD_DIM = 16
EPS_LN = 1e-5
EPS_Z = 1e-8
CAPACITY_FACTOR = 1.25
FAR = 1.0e6
C_GATE, C_ID, C_MEAN, C_RSTD, EXTRA = 0, 1, 2, 3, 4


def macaron_kernel(nc, x, Wq, bq, Wk, bk, Wv, bv, Wo, bo, R, wg, w1, b1, w2, b2, out):
    NBAT, SEQ, D = x.shape
    E, _, F = w1.shape
    T = NBAT * SEQ
    KD = D // P
    NJ = SEQ // P
    FM = F // P
    CAP = int(CAPACITY_FACTOR * T / E)
    NS = CAP // P
    HALF = CAP // 2
    SLOTS = E * CAP
    ROW = D + EXTRA
    QSCALE = 1.0 / float(HEAD_DIM) ** 0.5
    GT, ID, MEAN, RSTD = D + C_GATE, D + C_ID, D + C_MEAN, D + C_RSTD

    x_rows = x.rearrange("b s d -> (b s) d")
    out_rows = out.rearrange("b s d -> (b s) d")
    x1_rows = nc.dram_tensor("x1_rows", [T, D], F32).ap()
    routed = [nc.dram_tensor(f"routed{i}", [SLOTS, ROW], F32).ap() for i in range(2)]
    after_ffn = [x1_rows, out_rows]

    with ExitStack() as ctx:
        def sb(name, shape, dt=F32):
            return ctx.enter_context(nc.sbuf_tensor(name, shape, dt))

        def sem(name):
            return ctx.enter_context(nc.semaphore(name))

        def sem2(name):
            return [sem(f"{name}_even"), sem(f"{name}_odd")]

        ident = sb("ident", [P, P])
        ones = sb("ones", [P, P])
        upto = sb("upto", [P, P])
        same_head = sb("same_head", [P, P])
        minus_half_head = sb("minus_half_head", [P, P])
        rank_i = sb("rank_i", [P, E], I32)
        rank = sb("rank", [P, E])
        ids_i = sb("ids_i", [P, T // P], I32)
        ids = sb("ids", [P, T // P])
        exponent = sb("exponent", [P, NJ])
        eps = sb("eps", [P, NJ])
        filler = sb("filler", [P, 1, ROW])
        w_raw = sb("w_raw", [P, 4, KD, D])
        wT = sb("wT", [P, 4, KD, D])
        wg_sb = sb("wg_sb", [P, KD, E])
        r_heads = sb("r_heads", [P, P])
        bias_rows = sb("bias_rows", [E * FM + 2 * KD, P])
        bias_cols = sb("bias_cols", [P, E * FM + 2 * KD])
        qk_bias = sb("qk_bias", [P, 2 * KD])
        bv_sb = sb("bv_sb", [P, 1, D])
        bo_sb = sb("bo_sb", [P, 1, D])
        b2_sb = sb("b2_sb", [P, E, D])
        rows = [sb(f"rows{i}", [P, NJ, ROW]) for i in range(2)]
        r_st = sb("r_st", [P, NJ, 6])
        r_xn = [sb(f"r_xn{i}", [P, NJ, D]) for i in range(2)]
        r_xT = sb("r_xT", [P, KD, SEQ])
        r_top = sb("r_top", [P, NJ])
        r_eq = sb("r_eq", [P, NJ, E])
        r_dl = sb("r_dl", [P, NJ, E])
        r_sc = sb("r_sc", [P, NJ, E])
        r_best = [sb(f"r_best{i}", [P, NJ]) for i in range(2)]
        r_oh = [sb(f"r_oh{i}", [P, NJ, E]) for i in range(2)]
        r_seen = [sb(f"r_seen{i}", [P, NJ, E]) for i in range(2)]
        r_ex = sb("r_ex", [P, NJ, E])
        r_sum = sb("r_sum", [P, NJ])
        r_inv = sb("r_inv", [P, NJ])
        r_pm = sb("r_pm", [P, NJ, E])
        r_pos = sb("r_pos", [P, NJ])
        r_slot = sb("r_slot", [P, NJ])
        r_over = sb("r_over", [P, NJ])
        r_idx = [sb(f"r_idx{i}", [P, NJ], I32) for i in range(2)]
        w1_sb = [sb(f"w1_sb{i}", [P, KD, F]) for i in range(2)]
        w2_sb = [sb(f"w2_sb{i}", [P, FM, D]) for i in range(2)]
        xe = [sb(f"xe{i}", [P, NS, ROW]) for i in range(2)]
        xs = sb("xs", [P, NS, D])
        xT = [sb(f"xT{i}", [P, KD, CAP]) for i in range(2)]
        hT = sb("hT", [P, FM, CAP])
        y_b = sb("y_b", [P, 2, D])
        y_rows = [sb(f"y_rows{i}", [P, NS, D]) for i in range(2)]
        y_idx = [sb(f"y_idx{i}", [P, NS], I32) for i in range(2)]
        x1 = [sb(f"x1_{i}", [P, NJ, D]) for i in range(2)]
        a_st = sb("a_st", [P, NJ, 6])
        a_mv = sb("a_mv", [P, NJ, 2])
        a_xn = sb("a_xn", [P, NJ, D])
        a_xT = sb("a_xT", [P, KD, SEQ])
        xb = [sb(f"xb{i}", [P, NJ, D]) for i in range(2)]
        spare = hT[:, :, :].rearrange("p m t -> p (m t)")
        assert FM * CAP >= (2 * KD + 3 * KD) * SEQ

        def in_spare(block, n):
            return spare[:, block * SEQ:(block + n) * SEQ].rearrange("p (k t) -> p k t", k=n)

        qk = w_raw[:, :, :, :].rearrange("p w m d -> p (w m d)").rearrange("p (k t) -> p k t", k=2 * KD)
        qk2 = in_spare(0, 2 * KD)
        kf = in_spare(2 * KD, KD)
        zt = in_spare(3 * KD, KD)
        oT = in_spare(4 * KD, KD)
        qf = [sb(f"qf{i}", [P, KD, SEQ]) for i in range(2)]
        zr = [sb(f"zr{i}", [P, KD, SEQ]) for i in range(2)]
        kt = [sb(f"kt{i}", [P, NJ, D]) for i in range(2)]
        vt = [sb(f"vt{i}", [P, NJ, D]) for i in range(2)]
        kv = sb("kv", [P, KD, P])

        ps = ctx.enter_context(nc.psum_tensor("ps", [P, 8, 512], F32))

        def feat_banks(b):
            return ps[:, b:b + 2, :]

        def tok_banks(b):
            return ps[:, b:b + 2, :].rearrange("p b (j d) -> p (b j) d", d=D)

        s_const = sem("s_const")
        s_zero = sem("s_zero")
        s_rzero = sem("s_rzero")
        s_wload = sem("s_wload")
        s_rload = sem("s_rload")
        s_bload = sem("s_bload")
        s_fill = sem2("s_fill")
        s_base = sem("s_base")
        s_wT_pe = sem("s_wT_pe")
        s_wT = sem("s_wT")
        s_qkb = sem("s_qkb")
        s_rx = sem2("s_rx")
        s_x2 = sem("s_x2")
        s_rst = sem("s_rst")
        s_rvar = sem("s_rvar")
        s_rve = sem("s_rve")
        s_rrs = sem("s_rrs")
        s_rid = sem("s_rid")
        s_rxn = sem("s_rxn")
        s_rtp = sem("s_rtp")
        s_rxT = sem("s_rxT")
        s_rlg = sem("s_rlg")
        s_rtop = sem("s_rtop")
        s_req = sem("s_req")
        s_rdl = sem("s_rdl")
        s_rsc = sem("s_rsc")
        s_rbest = sem("s_rbest")
        s_roh = sem("s_roh")
        s_rseen = sem("s_rseen")
        s_rex = sem("s_rex")
        s_rsum = sem("s_rsum")
        s_rinv = sem("s_rinv")
        s_rgate = sem("s_rgate")
        s_rcnt = sem("s_rcnt")
        s_rpm = sem("s_rpm")
        s_rpos = sem("s_rpos")
        s_rslot = sem("s_rslot")
        s_rover = sem("s_rover")
        s_ridx = sem("s_ridx")
        s_rscat = sem2("s_rscat")
        s_keep = sem2("s_keep")
        s_w1 = sem2("s_w1")
        s_w2 = sem2("s_w2")
        s_xe = sem2("s_xe")
        s_xs = sem("s_xs")
        s_yid = sem("s_yid")
        s_xtp = sem("s_xtp")
        s_xT = sem("s_xT")
        s_h = sem("s_h")
        s_relu = sem("s_relu")
        s_y = sem("s_y")
        s_yb = sem("s_yb")
        s_yrow = sem("s_yrow")
        s_yscat = sem2("s_yscat")
        s_ax = sem2("s_ax")
        s_ast = sem("s_ast")
        s_avar = sem("s_avar")
        s_ave = sem("s_ave")
        s_ars = sem("s_ars")
        s_axn = sem("s_axn")
        s_xb = sem("s_xb")
        s_atp = sem("s_atp")
        s_axT = sem("s_axT")
        s_qkps = sem("s_qkps")
        s_qk = sem("s_qk")
        s_qk2 = sem("s_qk2")
        s_vps = sem("s_vps")
        s_v = sem("s_v")
        s_fps = sem("s_fps")
        s_f = sem("s_f")
        s_zps = sem("s_zps")
        s_zt = sem("s_zt")
        s_z = sem("s_z")
        s_ktps = sem("s_ktps")
        s_kt = sem("s_kt")
        s_kvps = sem("s_kvps")
        s_kv = sem("s_kv")
        s_ops = sem("s_ops")
        s_o = sem("s_o")
        s_yps = sem("s_yps")

        s_aggr_go = sem("s_aggr_go")
        s_scatter_go = sem("s_scatter_go")

        N_CONST = 12
        ALL_ROUTED = 16 * NJ * NBAT // 2
        ALL_SLOTS = 16 * NS * E // 2

        def steps(eng, first, loop_from, loop_to, last, body):
            for n in range(first, loop_from):
                body(n, n // 2, n)
            with eng.Fori(0, (loop_to - loop_from) // 2) as i:
                for u in range(2):
                    body(loop_from + u + 2 * i, loop_from // 2 + i, loop_from + u)
            for n in range(loop_to, last):
                body(n, n // 2, n)

        block = ctx.enter_context(nc.Block())

        @block.sync
        def _(sp):
            def load_rows(n, h, r):
                if r >= 2:
                    sp.wait_ge(s_rscat[r % 2], 16 * NJ * h)
                sp.dma_start(rows[r % 2][:, :, 0:D],
                             x_rows[bass.ds(n * SEQ, SEQ), :].rearrange("(j p) d -> p j d", p=P)
                             ).then_inc(s_rx[r % 2], 16)

            def fill(ph):
                sp.dma_start(routed[ph].rearrange("(n p) d -> p n d", p=P),
                             filler[:, :, :].to_broadcast([P, SLOTS // P, ROW])).then_inc(s_fill[ph], 16)

            def load_weights(n, h, r):
                e = n - (r // E) * E
                if r >= 2:
                    sp.wait_ge(s_h, FM * (n - 1))
                sp.dma_start(w1_sb[r % 2][:, :, :],
                             w1[bass.ds(e, 1), :, :].rearrange("e (k p) f -> p (e k) f", p=P)
                             ).then_inc(s_w1[r % 2], 16)
                if r >= 2:
                    sp.wait_ge(s_y, NS * (n - 1))
                sp.dma_start(w2_sb[r % 2][:, :, :],
                             w2[bass.ds(e, 1), :, :].rearrange("e (m p) d -> p (e m) d", p=P)
                             ).then_inc(s_w2[r % 2], 16)

            def load_slots(n, h, r):
                ph = r // E
                if r >= 2:
                    sp.wait_ge(s_yrow, NS * (n - 1))
                    sp.wait_ge(s_yid, n - 1)
                sp.dma_start(xe[r % 2][:, :, :],
                             routed[ph][bass.ds((n - ph * E) * CAP, CAP), :].rearrange("(s p) d -> p s d", p=P)
                             ).then_inc(s_xe[r % 2], 16)

            def load_both(n, h, r):
                load_weights(n, h, r)
                load_slots(n, h, r)

            load_rows(0, 0, 0)
            for i, w in enumerate((Wq, Wk, Wv, Wo)):
                sp.dma_start(w_raw[:, i, :, :], w.rearrange("(m p) d -> p m d", p=P)).then_inc(s_wload, 16)
            sp.dma_start(bias_rows[0:E * FM, :], b1.rearrange("e (m p) -> (e m) p", p=P)).then_inc(s_wload, 16)
            for i, b in enumerate((bq, bk)):
                lo = E * FM + i * KD
                sp.dma_start(bias_rows[lo:lo + KD, :], b.rearrange("(m p) -> m p", p=P)).then_inc(s_wload, 16)
            sp.dma_start(wg_sb[:, :, :], wg.rearrange("(k p) e -> p k e", p=P)).then_inc(s_bload, 16)
            load_rows(1, 0, 1)
            sp.wait_ge(s_const, N_CONST)
            fill(0)
            steps(sp, 2, 2, NBAT, NBAT, load_rows)
            load_weights(0, 0, 0)
            load_weights(1, 0, 1)
            sp.dma_start(bv_sb[:, 0, :], bv.rearrange("(a d) -> a d", a=1).to_broadcast([P, D])).then_inc(s_bload, 16)
            sp.dma_start(bo_sb[:, 0, :], bo.rearrange("(a d) -> a d", a=1).to_broadcast([P, D])).then_inc(s_bload, 16)
            sp.dma_start(b2_sb[:, :, :].rearrange("p e d -> p (e d)"),
                         b2.rearrange("(a e) d -> a (e d)", a=1).to_broadcast([P, E * D])).then_inc(s_bload, 16)
            sp.wait_ge(s_rzero, 1)
            for hd in range(P // HEAD_DIM):
                at = slice(hd * HEAD_DIM, (hd + 1) * HEAD_DIM)
                sp.dma_start(r_heads[at, at], R).then_inc(s_rload, 16)
            sp.dma_start(x1_rows, x_rows).then_inc(s_base, 16)
            for q in s_rscat:
                sp.wait_ge(q, ALL_ROUTED)
            load_slots(0, 0, 0)
            load_slots(1, 0, 1)
            fill(1)
            steps(sp, 2, 2, E, E, load_both)

            def load_x1(n, h, r):
                if r >= 2:
                    sp.wait_ge(s_axn, n - 1)
                    sp.wait_ge(s_xb, n - 1)
                sp.dma_start(x1[r % 2][:, :, :],
                             x1_rows[bass.ds(n * SEQ, SEQ), :].rearrange("(j p) d -> p j d", p=P)
                             ).then_inc(s_ax[r % 2], 16)

            def store_x2(n, h, r):
                sp.wait_ge(s_x2, n + 1)
                sp.dma_start(out_rows[bass.ds(n * SEQ, SEQ), :].rearrange("(j p) d -> p j d", p=P),
                             rows[r % 2][:, :, 0:D]).then_inc(s_keep[r % 2], 16)

            for q in s_yscat:
                sp.wait_ge(q, ALL_SLOTS)
            load_x1(0, 0, 0)
            load_x1(1, 0, 1)
            load_weights(E, E // 2, E)
            load_weights(E + 1, E // 2, E + 1)

            def attention_traffic(n, h, r):
                load_x1(n, h, r)
                store_x2(n - 2, h - 1, r - 2)

            steps(sp, 2, 2, NBAT, NBAT, attention_traffic)
            store_x2(NBAT - 2, NBAT // 2 - 1, NBAT - 2)
            store_x2(NBAT - 1, NBAT // 2 - 1, NBAT - 1)
            for q in s_rscat:
                sp.wait_ge(q, 2 * ALL_ROUTED)
            load_slots(E, E // 2, E)
            load_slots(E + 1, E // 2, E + 1)
            steps(sp, E + 2, E + 2, 2 * E, 2 * E, load_both)
            for q in s_keep:
                sp.wait_ge(q, 16 * NBAT // 2)
            for q in s_yscat:
                sp.wait_ge(q, 2 * ALL_SLOTS)

        @block.gpsimd
        def _(pool):
            pool.memset(filler[:, :, :], 0.0).then_inc(s_const, 1)
            pool.memset(ident[:, :], 0.0).then_inc(s_const, 1)
            pool.memset(ones[:, :], 1.0).then_inc(s_const, 1)
            pool.memset(exponent[:, :], -0.5).then_inc(s_const, 1)
            pool.memset(eps[:, :], EPS_LN).then_inc(s_const, 1)
            pool.iota(rank_i[:, :], pattern=[[-1, E]], base=E, channel_multiplier=0).then_inc(s_const, 1)
            pool.iota(ids_i[:, :], pattern=[[P, T // P]], base=0, channel_multiplier=1).then_inc(s_const, 1)
            pool.wait_ge(s_const, 7)
            pool.memset(filler[:, :, ID:ID + 1], FAR).then_inc(s_const, 1)
            pool.affine_select(out=ident[:, :], in_=ident[:, :], compare_op=ALU.not_equal, fill=1.0,
                               base=0, pattern=[[-1, P]], channel_multiplier=1).then_inc(s_const, 1)
            pool.affine_select(out=upto[:, :], in_=ones[:, :], compare_op=ALU.is_ge, fill=0.0,
                               base=0, pattern=[[1, P]], channel_multiplier=-1).then_inc(s_const, 1)
            nh = P // HEAD_DIM
            pool.affine_select(out=minus_half_head[:, :], in_=ones[:, :], compare_op=ALU.is_ge, fill=0.0,
                               base=0, pattern=[[-HEAD_DIM, nh], [0, HEAD_DIM]],
                               channel_multiplier=1).then_inc(s_const, 1)
            pool.tensor_copy(ids[:, :], ids_i[:, :]).then_inc(s_const, 1)
            assert N_CONST == 12
            pool.wait_ge(s_const, N_CONST)
            pool.tensor_copy(rank[:, :], rank_i[:, :]).then_inc(s_const, 1)
            pool.affine_select(out=same_head[:, :], in_=minus_half_head[:, :], compare_op=ALU.is_ge, fill=0.0,
                               base=HEAD_DIM - 1, pattern=[[HEAD_DIM, nh], [0, HEAD_DIM]],
                               channel_multiplier=-1).then_inc(s_const, 1)
            pool.wait_ge(s_const, N_CONST + 2)
            pool.tensor_scalar(minus_half_head[:, :], same_head[:, :], -0.5, None, ALU.mult).then_inc(s_const, 1)

            def route_rstd(n, h, r):
                at = rows[r % 2][:, :, RSTD:RSTD + 1]
                pool.wait_ge(s_rvar, n + 1)
                pool.tensor_tensor(at, at, eps[:, :, None], ALU.add).then_inc(s_rve, 1)
                pool.wait_ge(s_rve, n + 1)
                pool.tensor_tensor(at, at, exponent[:, :, None], ALU.pow).then_inc(s_rrs, 1)

            def route_scatter(n, h, r):
                ph = r // NBAT
                pool.wait_ge(s_fill[ph], 16)
                pool.wait_ge(s_ridx, n + 1)
                pool.wait_ge(s_rgate, n + 1)
                pool.wait_ge(s_rid, n + 1)
                pool.wait_ge(s_rrs, n + 1)
                pool.sem_inc(s_scatter_go, 1)
                for j in range(NJ):
                    pool.indirect_dma_start(routed[ph], bass.IndirectOffsetOnAxis(ap=r_idx[r % 2][:, j:j + 1], axis=0),
                                            rows[r % 2][:, j, :], None, bounds_check=SLOTS - 1,
                                            oob_is_err=False).then_inc(s_rscat[r % 2], 16)

            def route(n, h, r):
                if r < NBAT:
                    route_rstd(n, h, r)
                if r >= 1:
                    route_scatter(n - 1, h - 1 if r % 2 == 0 else h, r - 1)

            steps(pool, 0, 2, NBAT, NBAT + 1, route)

            def slots_out(n, h, r):
                ph = r // E
                pool.wait_ge(s_yid, n + 1)
                for s in range(NS):
                    pool.wait_ge(s_yrow, NS * n + s + 1)
                    pool.sem_inc(s_scatter_go, 1)
                    pool.indirect_dma_start(after_ffn[ph],
                                            bass.IndirectOffsetOnAxis(ap=y_idx[r % 2][:, s:s + 1], axis=0),
                                            y_rows[r % 2][:, s, :], None, bounds_check=T - 1,
                                            oob_is_err=False).then_inc(s_yscat[r % 2], 16)

            pool.wait_ge(s_base, 16)
            steps(pool, 0, 0, E, E, slots_out)

            def add_bo(n, h, r):
                pool.wait_ge(s_ax[r % 2], 16 * (h + 1))
                if r >= 2:
                    pool.wait_ge(s_x2, n - 1)
                pool.tensor_tensor(xb[r % 2][:, :, :], x1[r % 2][:, :, :],
                                   bo_sb[:, :, :].to_broadcast([P, NJ, D]), ALU.add).then_inc(s_xb, 1)

            def norm_rstd(n, h, r):
                at = a_mv[:, :, 1:2]
                pool.wait_ge(s_avar, n + 1)
                pool.tensor_tensor(at, at, eps[:, :, None], ALU.add).then_inc(s_ave, 1)
                pool.wait_ge(s_ave, n + 1)
                pool.tensor_tensor(at, at, exponent[:, :, None], ALU.pow).then_inc(s_ars, 1)

            def attend(n, h, r):
                hb = h - 1 if r % 2 == 0 else h
                if r < NBAT:
                    add_bo(n, h, r)
                if r >= 1:
                    route_rstd(NBAT + n - 1, NBAT // 2 + hb, NBAT + r - 1)
                if r < NBAT - 1:
                    norm_rstd(n + 1, h, r + 1)
                if r >= 1:
                    route_scatter(NBAT + n - 1, NBAT // 2 + hb, NBAT + r - 1)

            pool.wait_ge(s_bload, 64)
            norm_rstd(0, 0, 0)
            steps(pool, 0, 2, NBAT - 2, NBAT + 1, attend)
            for q in s_keep:
                pool.wait_ge(q, 16 * NBAT // 2)
            steps(pool, E, E, 2 * E, 2 * E, slots_out)

        @block.scalar
        def _(act):
            for i in range(4):
                act.wait_ge(s_wT_pe, i + 1)
                nc.scalar.copy(wT[:, i, :, :].rearrange("p k d -> p (k d)"), ps[:, i, :]).then_inc(s_wT, 1)
            act.wait_ge(s_wT_pe, 5)
            nc.scalar.copy(bias_cols[:, :], ps[:, 4, 0:E * FM + 2 * KD]).then_inc(s_wT, 1)
            act.wait_ge(s_wT, 5)
            nc.scalar.mul(qk_bias[:, :], bias_cols[:, E * FM:], QSCALE).then_inc(s_qkb, 1)

            def route_evacuate(n, h, r):
                b = 0 if r < NBAT else 2
                act.wait_ge(s_rtp, n + 1)
                if r >= 1:
                    act.wait_ge(s_rlg, n)
                nc.scalar.copy(r_xT[:, :, :], feat_banks(b)).then_inc(s_rxT, 1)

            def route_exp(n, h, r):
                act.wait_ge(s_rdl, n + 1)
                if r >= 1:
                    act.wait_ge(s_rsum, n)
                nc.scalar.activation(r_ex[:, :, :], r_dl[:, :, :], ACT.Exp).then_inc(s_rex, 1)

            def route(n, h, r):
                if r >= 1:
                    route_exp(n - 1, h, r - 1)
                if r < NBAT:
                    route_evacuate(n, h, r)

            steps(act, 0, 2, NBAT, NBAT + 1, route)

            def slots_T(n, h, r):
                for c in range((NS + 1) // 2):
                    w = min(2, NS - 2 * c) * P
                    act.wait_ge(s_xtp, 3 * n + c + 1)
                    if c == 0 and r >= 2:
                        act.wait_ge(s_h, FM * (n - 1))
                    nc.scalar.copy(xT[r % 2][:, :, 2 * c * P:2 * c * P + w],
                                   ps[:, 6 + c % 2, :].rearrange("p (k t) -> p k t", k=KD)[:, :, 0:w]
                                   ).then_inc(s_xT, 1)

            def relu(n, h, r):
                if r >= 1:
                    act.wait_ge(s_y, NS * n)
                for m in range(FM):
                    act.wait_ge(s_h, FM * n + m + 1)
                    b = 2 * (m % 2)
                    nc.scalar.activation(hT[:, m, :].rearrange("p (a t) -> p a t", a=2), ps[:, b:b + 2, 0:HALF],
                                         ACT.Relu, bias=bias_cols[:, bass.ds((n - (r // E) * E) * FM + m, 1)]
                                         ).then_inc(s_relu, 1)

            def expert(n, h, r):
                relu(n, h, r)
                if r % E != E - 1:
                    slots_T(n + 1, h, r + 1)

            slots_T(0, 0, 0)
            steps(act, 0, 2, E - 2, E, expert)

            def attend(n, h, r):
                if r < NBAT:
                    act.wait_ge(s_atp, n + 1)
                    if r >= 1:
                        act.wait_ge(s_vps, n)
                    nc.scalar.copy(a_xT[:, :, :], feat_banks(0)).then_inc(s_axT, 1)
                    for c in range(2 * KD):
                        act.wait_ge(s_qk, 2 * KD * n + c + 1)
                        if c == 0 and r >= 1:
                            act.wait_ge(s_fps, 2 * KD * n)
                        nc.scalar.activation(qk2[:, c, :], qk[:, c, :], ACT.Square).then_inc(s_qk2, 1)
                    for c in range(2 * KD):
                        act.wait_ge(s_fps, 2 * KD * n + c + 1)
                        if c == 0 and r >= 2:
                            act.wait_ge(s_ops, n - 1)
                        if c == KD and r >= 1:
                            act.wait_ge(s_ktps, n)
                        dst = qf[r % 2][:, c, :] if c < KD else kf[:, c - KD, :]
                        nc.scalar.activation(dst, ps[:, 4 + c, :], ACT.Exp).then_inc(s_f, 1)
                if r >= 1:
                    route_evacuate(NBAT + n - 1, h, NBAT + r - 1)
                if r < NBAT:
                    act.wait_ge(s_ktps, n + 1)
                    if r >= 2:
                        act.wait_ge(s_kvps, n - 1)
                    nc.scalar.copy(kt[r % 2][:, :, :], tok_banks(6)).then_inc(s_kt, 1)
                if r >= 1:
                    route_exp(NBAT + n - 1, h, NBAT + r - 1)

            steps(act, 0, 2, NBAT - 2, NBAT + 1, attend)
            slots_T(E, E // 2, E)
            steps(act, E, E, 2 * E - 2, 2 * E, expert)

        @block.tensor
        def _(pe):
            pe.wait_ge(s_const, N_CONST)
            pe.wait_ge(s_wload, 16 * 7)
            for i in range(4):
                for k in range(KD):
                    for m in range(KD):
                        mm = nc.tensor.transpose(ps[:, i, k * D + m * P:k * D + (m + 1) * P],
                                                 w_raw[:, i, m, k * P:(k + 1) * P], ident[:, :])
                mm.then_inc(s_wT_pe, 1)
            nb = E * FM + 2 * KD
            nc.tensor.transpose(ps[:, 4, 0:nb], bias_rows[:, :], ident[0:nb, 0:nb]).then_inc(s_wT_pe, 1)
            pe.wait_ge(s_wT, 5)
            pe.wait_ge(s_bload, 16)

            def rows_T(n, h, r):
                b = 0 if r < NBAT else 2
                pe.wait_ge(s_rxn, n + 1)
                if r % NBAT:
                    pe.wait_ge(s_rxT, n)
                for j in range(NJ):
                    for k in range(KD):
                        mm = nc.tensor.transpose(ps[:, b + k, j * P:(j + 1) * P],
                                                 r_xn[r % 2][:, j, k * P:(k + 1) * P], ident[:, :])
                mm.then_inc(s_rtp, 1)

            def logits(n, h, r):
                pe.wait_ge(s_rxT, n + 1)
                if r >= 1:
                    pe.wait_ge(s_rdl, n)
                    pe.wait_ge(s_req, n)
                for j in range(NJ):
                    for k in range(KD):
                        mm = nc.tensor.matmul(ps[:, 4, j * E:(j + 1) * E], r_xT[:, k, j * P:(j + 1) * P],
                                              wg_sb[:, k, :], start=(k == 0), stop=(k == KD - 1))
                mm.then_inc(s_rlg, 1)

            def counts(n, h, r):
                pe.wait_ge(s_roh, n + 1)
                pe.wait_ge(s_rseen, NJ * (n + 1))
                if r >= 1:
                    pe.wait_ge(s_rpm, n)
                dst = ps[:, 5, 0:NJ * E]
                nc.tensor.matmul(dst, upto[:, :], r_oh[r % 2][:, :, :].rearrange("p j e -> p (j e)"),
                                 start=True, stop=False)
                nc.tensor.matmul(dst, ones[:, :], r_seen[r % 2][:, :, :].rearrange("p j e -> p (j e)"),
                                 start=False, stop=True).then_inc(s_rcnt, 1)

            def route(n, h, r):
                if r >= 1:
                    logits(n - 1, h, r - 1)
                if r < NBAT:
                    rows_T(n, h, r)
                if r >= 1:
                    counts(n - 1, h, r - 1)

            steps(pe, 0, 2, NBAT, NBAT + 1, route)

            def slots_T(n, h, r):
                pe.wait_ge(s_xs, n + 1)
                for c in range((NS + 1) // 2):
                    if r >= 1 or c >= 2:
                        pe.wait_ge(s_xT, 3 * n + c - 1)
                    for s in range(2 * c, min(2 * c + 2, NS)):
                        for k in range(KD):
                            at = k * 2 * P + (s - 2 * c) * P
                            mm = nc.tensor.transpose(ps[:, 6 + c % 2, at:at + P],
                                                     xs[:, s, k * P:(k + 1) * P], ident[:, :])
                    mm.then_inc(s_xtp, 1)

            def hidden(n, h, r):
                pe.wait_ge(s_xT, 3 * n + 3)
                pe.wait_ge(s_w1[r % 2], 16 * (h + 1))
                for m in range(FM):
                    if r >= 1 or m >= 2:
                        pe.wait_ge(s_relu, FM * n + m - 1)
                    b = 2 * (m % 2)
                    for k in range(KD):
                        for a in range(2):
                            mm = nc.tensor.matmul(ps[:, b + a, 0:HALF], w1_sb[r % 2][:, k, m * P:(m + 1) * P],
                                                  xT[r % 2][:, k, a * HALF:(a + 1) * HALF],
                                                  start=(k == 0), stop=(k == KD - 1))
                    mm.then_inc(s_h, 1)

            def expert_out(n, h, r):
                pe.wait_ge(s_relu, FM * (n + 1))
                pe.wait_ge(s_w2[r % 2], 16 * (h + 1))
                for s in range(NS):
                    if r >= 1 or s >= 2:
                        pe.wait_ge(s_yb, NS * n + s - 1)
                    b = 4 + s % 2 if r % 2 == 0 else 4 + (s + 1) % 2
                    for m in range(FM):
                        mm = nc.tensor.matmul(ps[:, b, 0:D], hT[:, m, s * P:(s + 1) * P], w2_sb[r % 2][:, m, :],
                                              start=(m == 0), stop=(m == FM - 1))
                    mm.then_inc(s_y, 1)

            def expert(n, h, r):
                hidden(n, h, r)
                if r % E != E - 1:
                    slots_T(n + 1, h, r + 1)
                expert_out(n, h, r)

            slots_T(0, 0, 0)
            steps(pe, 0, 2, E - 2, E, expert)

            def attend(n, h, r):
                early, late = r < NBAT, r >= 1
                hb = h
                nb_, rb = n - 1, r - 1
                if early:
                    pe.wait_ge(s_axn, n + 1)
                    if r >= 1:
                        pe.wait_ge(s_zt, n)
                    for j in range(NJ):
                        for k in range(KD):
                            mm = nc.tensor.transpose(ps[:, k, j * P:(j + 1) * P],
                                                     a_xn[:, j, k * P:(k + 1) * P], ident[:, :])
                    mm.then_inc(s_atp, 1)
                if late:
                    pe.wait_ge(s_kt, nb_ + 1)
                    pe.wait_ge(s_v, nb_ + 1)
                    if rb >= 1:
                        pe.wait_ge(s_rxT, NBAT + nb_)
                    for m in range(KD):
                        for j in range(NJ):
                            mm = nc.tensor.matmul(ps[:, 2, m * P:(m + 1) * P],
                                                  kt[rb % 2][:, j, m * P:(m + 1) * P],
                                                  vt[rb % 2][:, j, m * P:(m + 1) * P],
                                                  start=(j == 0), stop=(j == NJ - 1))
                    mm.then_inc(s_kvps, 1)
                if early:
                    pe.wait_ge(s_axT, n + 1)
                    if r >= 2:
                        pe.wait_ge(s_rdl, NBAT + n - 1)
                        pe.wait_ge(s_req, NBAT + n - 1)
                        pe.wait_ge(s_rpm, NBAT + n - 1)
                    if r >= 1:
                        pe.wait_ge(s_kt, n)
                    for c in range(2 * KD):
                        w, m = c // KD, c % KD
                        for k in range(KD):
                            mm = nc.tensor.matmul(ps[:, 4 + c, :], wT[:, w, k, m * P:(m + 1) * P], a_xT[:, k, :],
                                                  start=(k == 0), stop=(k == KD - 1))
                        mm.then_inc(s_qkps, 1)
                if late:
                    pe.wait_ge(s_kv, nb_ + 1)
                    if early:
                        pe.wait_ge(s_axT, n + 1)
                    pe.wait_ge(s_z, nb_ + 1)
                    for m in range(KD):
                        mm = nc.tensor.matmul(ps[:, m, :], kv[:, m, :], qf[rb % 2][:, m, :], start=True, stop=True)
                    mm.then_inc(s_ops, 1)
                if early:
                    for j in range(NJ):
                        for k in range(KD):
                            mm = nc.tensor.matmul(tok_banks(2)[:, j, :], a_xT[:, k, j * P:(j + 1) * P],
                                                  wT[:, 2, k, :], start=(k == 0), stop=(k == KD - 1))
                    mm.then_inc(s_vps, 1)
                if late:
                    pe.wait_ge(s_o, nb_ + 1)
                    for j in range(NJ):
                        for m in range(KD):
                            mm = nc.tensor.matmul(tok_banks(0)[:, j, :], oT[:, m, j * P:(j + 1) * P],
                                                  wT[:, 3, m, :], start=(m == 0), stop=(m == KD - 1))
                    mm.then_inc(s_yps, 1)
                if early:
                    for c in range(2 * KD):
                        pe.wait_ge(s_qk, 2 * KD * n + c + 1)
                        pe.wait_ge(s_qk2, 2 * KD * n + c + 1)
                        nc.tensor.matmul(ps[:, 4 + c, :], r_heads[:, :], qk[:, c, :], start=True, stop=False)
                        nc.tensor.matmul(ps[:, 4 + c, :], minus_half_head[:, :], qk2[:, c, :],
                                         start=False, stop=True).then_inc(s_fps, 1)
                    pe.wait_ge(s_f, 2 * KD * n + KD)
                    if late:
                        pe.wait_ge(s_x2, nb_ + 1)
                    for m in range(KD):
                        mm = nc.tensor.matmul(ps[:, m, :], same_head[:, :], qf[r % 2][:, m, :], start=True, stop=True)
                    mm.then_inc(s_zps, 1)
                if late:
                    if early:
                        pe.wait_ge(s_v, n + 1)
                    rows_T(NBAT + nb_, hb, NBAT + rb)
                if early:
                    pe.wait_ge(s_f, 2 * KD * (n + 1))
                    for j in range(NJ):
                        for m in range(KD):
                            mm = nc.tensor.transpose(tok_banks(6)[:, j, m * P:(m + 1) * P],
                                                     kf[:, m, j * P:(j + 1) * P], ident[:, :])
                    mm.then_inc(s_ktps, 1)
                if late:
                    logits(NBAT + nb_, hb, NBAT + rb)
                    counts(NBAT + nb_, hb, NBAT + rb)

            pe.wait_ge(s_const, N_CONST + 3)
            pe.wait_ge(s_rload, 16 * (P // HEAD_DIM))
            steps(pe, 0, 2, NBAT - 2, NBAT + 1, attend)
            slots_T(E, E // 2, E)
            steps(pe, E, E, 2 * E - 2, 2 * E, expert)

        @block.vector
        def _(dve):
            dve.memset(r_heads[:, :], 0.0).then_inc(s_rzero, 1)
            dve.memset(r_seen[0][:, 0, :], 0.0).then_inc(s_zero, 1)
            dve.wait_ge(s_const, N_CONST + 1)

            def route_stats(n, h, r):
                x_at = rows[r % 2]
                if r < NBAT:
                    dve.wait_ge(s_rx[r % 2], 16 * (h + 1))
                else:
                    dve.wait_ge(s_x2, n - NBAT + 1)
                if r >= 1:
                    dve.wait_ge(s_rvar, n)
                for j in range(NJ):
                    ins = nc.vector.bn_stats(r_st[:, j, :], x_at[:, j, 0:D])
                ins.then_inc(s_rst, 1)
                dve.wait_ge(s_rst, n + 1)
                nc.vector.tensor_copy(x_at[:, :, ID:ID + 1],
                                      ids[:, bass.ds((n - (r // NBAT) * NBAT) * NJ, NJ)][:, :, None]
                                      ).then_inc(s_rid, 1)
                for j in range(NJ):
                    ins = nc.vector.bn_aggr(x_at[:, j, MEAN:MEAN + 2], r_st[:, j, :])
                ins.then_inc(s_rvar, 1)

            def route_norm(n, h, r):
                x_at = rows[r % 2]
                dve.wait_ge(s_rrs, n + 1)
                if r >= 2:
                    dve.wait_ge(s_rtp, n - 1)
                for j in range(NJ):
                    ins = nc.vector.tensor_scalar(r_xn[r % 2][:, j, :], x_at[:, j, 0:D], x_at[:, j, MEAN:MEAN + 1],
                                                  x_at[:, j, RSTD:RSTD + 1], ALU.subtract, ALU.mult)
                ins.then_inc(s_rxn, 1)

            def route_choose(n, h, r):
                lg = ps[:, 4, 0:NJ * E].rearrange("p (j e) -> p j e", e=E)
                wide = [P, NJ, E]
                oh, seen, nxt, best = r_oh[r % 2], r_seen[r % 2], r_seen[1 - r % 2], r_best[r % 2]
                dve.wait_ge(s_rlg, n + 1)
                nc.vector.tensor_reduce(r_top[:, :], lg, AX.X, ALU.max).then_inc(s_rtop, 1)
                dve.wait_ge(s_rtop, n + 1)
                nc.vector.tensor_tensor(r_eq[:, :, :], lg, r_top[:, :, None].to_broadcast(wide),
                                        ALU.is_ge).then_inc(s_req, 1)
                if r >= 1:
                    dve.wait_ge(s_rex, n)
                nc.vector.tensor_tensor(r_dl[:, :, :], lg, r_top[:, :, None].to_broadcast(wide),
                                        ALU.subtract).then_inc(s_rdl, 1)
                dve.wait_ge(s_req, n + 1)
                nc.vector.tensor_tensor(r_sc[:, :, :], r_eq[:, :, :], rank[:, None, :].to_broadcast(wide),
                                        ALU.mult).then_inc(s_rsc, 1)
                dve.wait_ge(s_rsc, n + 1)
                nc.vector.tensor_reduce(best[:, :], r_sc[:, :, :], AX.X, ALU.max).then_inc(s_rbest, 1)
                dve.wait_ge(s_rbest, n + 1)
                if r >= 2:
                    dve.wait_ge(s_rcnt, n - 1)
                nc.vector.tensor_tensor(oh[:, :, :], r_sc[:, :, :], best[:, :, None].to_broadcast(wide),
                                        ALU.is_equal).then_inc(s_roh, 1)
                dve.wait_ge(s_roh, n + 1)
                if r == 0:
                    dve.wait_ge(s_zero, 1)
                if r == NBAT:
                    dve.wait_ge(s_rcnt, NBAT)
                    dve.wait_ge(s_rseen, NJ * NBAT)
                    nc.vector.memset(seen[:, 0, :], 0.0).then_inc(s_zero, 1)
                    dve.wait_ge(s_zero, 2)
                if r >= 1:
                    dve.wait_ge(s_rcnt, n)
                for j in range(NJ):
                    if r >= 1 or j >= 1:
                        dve.wait_ge(s_rseen, NJ * n + j)
                    dst = seen[:, j + 1, :] if j + 1 < NJ else nxt[:, 0, :]
                    nc.vector.tensor_tensor(dst, seen[:, j, :], oh[:, j, :], ALU.add).then_inc(s_rseen, 1)

            def route_place(n, h, r):
                x_at = rows[r % 2]
                dve.wait_ge(s_rex, n + 1)
                nc.vector.tensor_reduce(r_sum[:, :], r_ex[:, :, :], AX.X, ALU.add).then_inc(s_rsum, 1)
                dve.wait_ge(s_rsum, n + 1)
                nc.vector.reciprocal(r_inv[:, :], r_sum[:, :]).then_inc(s_rinv, 1)
                dve.wait_ge(s_rinv, n + 1)
                nc.vector.tensor_scalar(x_at[:, :, GT:GT + 1], r_inv[:, :, None], 0.5, None,
                                        ALU.mult).then_inc(s_rgate, 1)
                dve.wait_ge(s_rcnt, n + 1)
                nc.vector.tensor_tensor(r_pm[:, :, :], r_oh[r % 2][:, :, :],
                                        ps[:, 5, 0:NJ * E].rearrange("p (j e) -> p j e", e=E),
                                        ALU.mult).then_inc(s_rpm, 1)
                dve.wait_ge(s_rpm, n + 1)
                nc.vector.tensor_reduce(r_pos[:, :], r_pm[:, :, :], AX.X, ALU.add).then_inc(s_rpos, 1)
                dve.wait_ge(s_rpos, n + 1)
                nc.vector.scalar_tensor_tensor(out=r_slot[:, :], in0=r_best[r % 2][:, :], scalar=-float(CAP),
                                               in1=r_pos[:, :], op0=ALU.mult, op1=ALU.add).then_inc(s_rslot, 1)
                nc.vector.tensor_scalar(r_over[:, :], r_pos[:, :], float(CAP), FAR, ALU.is_gt,
                                        ALU.mult).then_inc(s_rover, 1)
                dve.wait_ge(s_rslot, n + 1)
                dve.wait_ge(s_rover, n + 1)
                if r >= 2:
                    dve.wait_ge(s_rscat[r % 2], 16 * NJ * h)
                nc.vector.scalar_tensor_tensor(out=r_idx[r % 2][:, :], in0=r_slot[:, :], scalar=float(SLOTS - 1),
                                               in1=r_over[:, :], op0=ALU.add, op1=ALU.add).then_inc(s_ridx, 1)

            def route(n, h, r):
                if r < NBAT:
                    route_stats(n, h, r)
                if r >= 1:
                    route_choose(n - 1, h, r - 1)
                if r < NBAT:
                    route_norm(n, h, r)
                if r >= 1:
                    route_place(n - 1, h - 1 if r % 2 == 0 else h, r - 1)

            steps(dve, 0, 2, NBAT, NBAT + 1, route)

            def slots_norm(n, h, r):
                at = xe[r % 2]
                dve.wait_ge(s_xe[r % 2], 16 * (h + 1))
                if r >= 1:
                    dve.wait_ge(s_xtp, 3 * n)
                for s in range(NS):
                    ins = nc.vector.tensor_scalar(xs[:, s, :], at[:, s, 0:D], at[:, s, MEAN:MEAN + 1],
                                                  at[:, s, RSTD:RSTD + 1], ALU.subtract, ALU.mult)
                ins.then_inc(s_xs, 1)
                if r >= 2:
                    dve.wait_ge(s_yscat[r % 2], 16 * NS * h)
                nc.vector.tensor_copy(y_idx[r % 2][:, :, None], at[:, :, ID:ID + 1]).then_inc(s_yid, 1)

            def slots_add(n, h, r):
                at = xe[r % 2]
                for s in range(NS):
                    q = s % 2 if r % 2 == 0 else (s + 1) % 2
                    dve.wait_ge(s_y, NS * n + s + 1)
                    if r >= 1 or s >= 2:
                        dve.wait_ge(s_yrow, NS * n + s - 1)
                    nc.vector.tensor_tensor(y_b[:, q, :], ps[:, 4 + q, 0:D],
                                            b2_sb[:, bass.ds(n - (r // E) * E, 1), :].rearrange("p e d -> p (e d)"),
                                            ALU.add).then_inc(s_yb, 1)
                    dve.wait_ge(s_yb, NS * n + s + 1)
                    nc.vector.scalar_tensor_tensor(out=y_rows[r % 2][:, s, :], in0=y_b[:, q, :],
                                                   scalar=at[:, s, GT:GT + 1], in1=at[:, s, 0:D],
                                                   op0=ALU.mult, op1=ALU.add).then_inc(s_yrow, 1)

            def expert(n, h, r):
                if r % E != E - 1:
                    slots_norm(n + 1, h if r % 2 == 0 else h + 1, r + 1)
                slots_add(n, h, r)

            dve.wait_ge(s_bload, 64)
            slots_norm(0, 0, 0)
            steps(dve, 0, 2, E - 2, E, expert)

            def norm_stats(n, h, r):
                dve.wait_ge(s_ax[r % 2], 16 * (h + 1))
                if r >= 1:
                    dve.wait_ge(s_avar, n)
                for j in range(NJ):
                    ins = nc.vector.bn_stats(a_st[:, j, :], x1[r % 2][:, j, :])
                ins.then_inc(s_ast, 1)
                dve.wait_ge(s_ast, n + 1)
                if r >= 1:
                    dve.wait_ge(s_axn, n)
                dve.sem_inc(s_aggr_go, 1)
                for j in range(NJ):
                    ins = nc.vector.bn_aggr(a_mv[:, j, :], a_st[:, j, :])
                ins.then_inc(s_avar, 1)

            def norm(n, h, r):
                dve.wait_ge(s_ars, n + 1)
                if r >= 1:
                    dve.wait_ge(s_atp, n)
                for j in range(NJ):
                    ins = nc.vector.tensor_scalar(a_xn[:, j, :], x1[r % 2][:, j, :], a_mv[:, j, 0:1],
                                                  a_mv[:, j, 1:2], ALU.subtract, ALU.mult)
                ins.then_inc(s_axn, 1)

            def attend(n, h, r):
                early, late = r < NBAT, r >= 1
                b, rb = n - 1, r - 1
                hb = h - 1 if r % 2 == 0 else h
                hn = h if r % 2 == 0 else h + 1
                if late:
                    dve.wait_ge(s_kvps, b + 1)
                    if rb >= 1:
                        dve.wait_ge(s_ops, b)
                    nc.vector.tensor_tensor(kv[:, :, :], ps[:, 2, 0:D].rearrange("p (m e) -> p m e", e=P),
                                            same_head[:, None, :].to_broadcast([P, KD, P]),
                                            ALU.mult).then_inc(s_kv, 1)
                if early:
                    for c in range(2 * KD):
                        dve.wait_ge(s_qkps, 2 * KD * n + c + 1)
                        if c == 0 and r >= 1:
                            dve.wait_ge(s_fps, 2 * KD * n)
                        nc.vector.tensor_scalar(qk[:, c, :], ps[:, 4 + c, :], QSCALE, qk_bias[:, c:c + 1],
                                                ALU.mult, ALU.add).then_inc(s_qk, 1)
                if late:
                    dve.wait_ge(s_ops, b + 1)
                    if rb >= 1:
                        dve.wait_ge(s_yps, b)
                    nc.vector.tensor_tensor(oT[:, :, :], feat_banks(0), zr[rb % 2][:, :, :],
                                            ALU.mult).then_inc(s_o, 1)
                if early:
                    dve.wait_ge(s_vps, n + 1)
                    if r >= 2:
                        dve.wait_ge(s_kvps, n - 1)
                    nc.vector.tensor_tensor(vt[r % 2][:, :, :], tok_banks(2), bv_sb[:, :, :].to_broadcast([P, NJ, D]),
                                            ALU.add).then_inc(s_v, 1)
                if late:
                    dve.wait_ge(s_yps, b + 1)
                    dve.wait_ge(s_xb, b + 1)
                    dve.wait_ge(s_rscat[rb % 2], ALL_ROUTED + 16 * NJ * hb)
                    if rb >= 2:
                        dve.wait_ge(s_keep[rb % 2], 16 * hb)
                    nc.vector.tensor_tensor(rows[rb % 2][:, :, 0:D], tok_banks(0), xb[rb % 2][:, :, :],
                                            ALU.add).then_inc(s_x2, 1)
                    route_stats(NBAT + b, NBAT // 2 + hb, NBAT + rb)
                if early:
                    dve.wait_ge(s_zps, n + 1)
                    if r >= 1:
                        dve.wait_ge(s_z, n)
                    nc.vector.tensor_scalar(zt[:, :, :], feat_banks(0), EPS_Z, None, ALU.add).then_inc(s_zt, 1)
                    dve.wait_ge(s_zt, n + 1)
                    if r >= 2:
                        dve.wait_ge(s_o, n - 1)
                    nc.vector.reciprocal(zr[r % 2][:, :, :], zt[:, :, :]).then_inc(s_z, 1)
                if late:
                    route_norm(NBAT + b, NBAT // 2 + hb, NBAT + rb)
                if r < NBAT - 1:
                    norm_stats(n + 1, hn, r + 1)
                if late:
                    route_choose(NBAT + b, NBAT // 2 + hb, NBAT + rb)
                if r < NBAT - 1:
                    norm(n + 1, hn, r + 1)
                if late:
                    route_place(NBAT + b, NBAT // 2 + hb, NBAT + rb)

            dve.wait_ge(s_const, N_CONST + 3)
            dve.wait_ge(s_qkb, 1)
            norm_stats(0, 0, 0)
            norm(0, 0, 0)
            steps(dve, 0, 2, NBAT - 2, NBAT + 1, attend)
            slots_norm(E, E // 2, E)
            steps(dve, E, E, 2 * E - 2, 2 * E, expert)


_INS = ["L0_attn_x", "L0_attn_Wq", "L0_attn_bq", "L0_attn_Wk", "L0_attn_bk", "L0_attn_Wv", "L0_attn_bv",
        "L0_attn_Wo", "L0_attn_bo", "L0_attn_R", "L0_ffn_wg", "L0_ffn_w1", "L0_ffn_b1", "L0_ffn_w2", "L0_ffn_b2"]
_OUTS = [((8, 512, 256), "float32")]


def kernel(**inputs):
    import numpy as _np
    import concourse.bacc as _bacc
    from concourse import mybir as _mybir
    from concourse.bass_utils import run_bass_kernel_spmd as _run

    nc = _bacc.Bacc("TRN2", target_bir_lowering=False, num_devices=1)
    arrays, args = {}, []
    for name in _INS:
        a = _np.ascontiguousarray(inputs[name])
        arrays[f"in_{name}_dram"] = a
        args.append(nc.dram_tensor(f"in_{name}_dram", a.shape, _mybir.dt.from_np(a.dtype), kind="ExternalInput").ap())
    for i, (shape, dtype) in enumerate(_OUTS):
        dt = _mybir.dt.from_np(_np.dtype(dtype))
        args.append(nc.dram_tensor(f"out_{i}_dram", shape, dt, kind="ExternalOutput").ap())
    macaron_kernel(nc, *args)
    r = _run(nc, [arrays], core_ids=[0])
    got = tuple(r.results[0][f"out_{i}_dram"] for i in range(len(_OUTS)))
    return got[0]
```

```python
from contextlib import ExitStack

import concourse.bass as bass
from concourse import mybir

F32 = mybir.dt.float32
BF16 = mybir.dt.bfloat16
F16 = mybir.dt.float16
I32 = mybir.dt.int32
ALU = mybir.AluOpType
ACT = mybir.ActivationFunctionType
AX = mybir.AxisListType

P = 128
HEAD_DIM = 16
EPS_LN = 1e-5
EPS_Z = 1e-8
CAPACITY_FACTOR = 1.25
FAR = 1.0e6
C_GATE, C_ID, C_SHIFT, C_RSTD, EXTRA = 0, 1, 2, 3, 4
W_SCALE, H_SCALE = 64.0, 8.0


def macaron_kernel(nc, x, Wq, bq, Wk, bk, Wv, bv, Wo, bo, R, wg, w1, b1, w2, b2, out):
    NBAT, SEQ, D = x.shape
    E, _, F = w1.shape
    T = NBAT * SEQ
    KD = D // P
    NJ = SEQ // P
    FM = F // P
    CAP = int(CAPACITY_FACTOR * T / E)
    NS = CAP // P
    HALF = CAP // 2
    SLOTS = E * CAP
    ROW = D + EXTRA
    QSCALE = 1.0 / float(HEAD_DIM) ** 0.5
    GT, ID, SHIFT, RSTD = D + C_GATE, D + C_ID, D + C_SHIFT, D + C_RSTD

    x_rows = x.rearrange("b s d -> (b s) d")
    out_rows = out.rearrange("b s d -> (b s) d")
    x1_rows = nc.dram_tensor("x1_rows", [T, D], F32).ap()
    routed = [nc.dram_tensor(f"routed{i}", [SLOTS, ROW], F32).ap() for i in range(2)]
    after_ffn = [x1_rows, out_rows]

    with ExitStack() as ctx:
        def sb(name, shape, dt=F32):
            return ctx.enter_context(nc.sbuf_tensor(name, shape, dt))

        def sem(name):
            return ctx.enter_context(nc.semaphore(name))

        def sem2(name):
            return [sem(f"{name}_even"), sem(f"{name}_odd")]

        ident = sb("ident", [P, P])
        ones = sb("ones", [P, P])
        ones_b = sb("ones_b", [P, P], BF16)
        upto = sb("upto", [P, P], BF16)
        same_head = sb("same_head", [P, P])
        minus_half_head = sb("minus_half_head", [P, P])
        head_cols = sb("head_cols", [P, P // HEAD_DIM])
        rank_i = sb("rank_i", [P, E], I32)
        rank = sb("rank", [P, E])
        ids_i = sb("ids_i", [P, T // P], I32)
        ids = sb("ids", [P, T // P])
        exponent = sb("exponent", [P, NJ])
        eps = sb("eps", [P, NJ])
        filler = sb("filler", [P, 1, ROW])
        w_raw = sb("w_raw", [P, 4, KD, D])
        wT_hi = sb("wT_hi", [P, 4, KD, D], F16)
        wT_lo = sb("wT_lo", [P, 4, KD, D], F16)
        wg_sb = sb("wg_sb", [P, KD, E])
        wg_hi = sb("wg_hi", [P, KD, E], F16)
        wg_lo = sb("wg_lo", [P, KD, E], F16)
        r_heads = sb("r_heads", [P, P])
        bias_rows = sb("bias_rows", [E * FM + 2 * KD, P])
        b1_cols = sb("b1_cols", [P, E * FM])
        qk_bias = sb("qk_bias", [P, 2 * KD])
        bv_sb = sb("bv_sb", [P, 1, D])
        bo_sb = sb("bo_sb", [P, 1, D])
        b2_sb = sb("b2_sb", [P, E, D])
        rows_first = sb("rows_first", [P, NBAT, NJ, ROW])
        rows = [sb(f"rows{i}", [P, NJ, ROW]) for i in range(2)]
        r_st = [sb(f"r_st{i}", [P, NJ, 6]) for i in range(2)]
        mv_first = sb("mv_first", [P, NBAT, NJ, 2])
        r_mv = [sb(f"r_mv{i}", [P, NJ, 2]) for i in range(2)]
        r_xn_both = sb("r_xn_both", [P, 2 * NJ * D])
        r_xn = [r_xn_both[:, i * NJ * D:(i + 1) * NJ * D].rearrange("p (j d) -> p j d", j=NJ) for i in range(2)]
        r_xT_hi = sb("r_xT_hi", [P, KD, SEQ], F16)
        r_xT_lo = sb("r_xT_lo", [P, KD, SEQ], F16)
        r_top = sb("r_top", [P, NJ])
        r_eq = sb("r_eq", [P, NJ, E])
        r_dl = sb("r_dl", [P, NJ, E])
        r_sc = sb("r_sc", [P, NJ, E])
        r_best = [sb(f"r_best{i}", [P, NJ]) for i in range(2)]
        r_oh = [sb(f"r_oh{i}", [P, NJ, E], BF16) for i in range(2)]
        r_sumj = sb("r_sumj", [P, E], BF16)
        r_seen = [sb(f"r_seen{i}", [P, 1, E], BF16) for i in range(2)]
        r_ex = sb("r_ex", [P, NJ, E])
        r_sum = sb("r_sum", [P, NJ])
        r_inv = sb("r_inv", [P, NJ])
        r_pm = sb("r_pm", [P, NJ, E])
        r_pos = sb("r_pos", [P, NJ])
        r_slot = sb("r_slot", [P, NJ])
        r_over = sb("r_over", [P, NJ])
        idx_first = sb("idx_first", [P, NBAT, NJ], I32)
        r_idx = [sb(f"r_idx{i}", [P, NJ], I32) for i in range(2)]
        w1_sb = [sb(f"w1_sb{i}", [P, KD, F]) for i in range(2)]
        w2_sb = [sb(f"w2_sb{i}", [P, FM, D]) for i in range(2)]
        xe = [sb(f"xe{i}", [P, NS, ROW]) for i in range(2)]
        xs = sb("xs", [P, NS, D])
        arena = sb("arena", [P, FM * CAP])

        def half_precision(words):
            halves = words.bitcast(F16)
            n = halves.shape[-1] // 2
            return [halves[:, i * n:(i + 1) * n] for i in range(2)]

        hT_hi, hT_lo = [v.rearrange("p (m t) -> p m t", m=FM) for v in half_precision(arena[:, :])]
        h_full = r_xn_both[:, 0:2 * CAP].rearrange("p (i t) -> p i t", i=2)
        xT_hi = sb("xT_hi", [P, KD, CAP], F16)
        xT_lo = sb("xT_lo", [P, KD, CAP], F16)
        w1_hi = sb("w1_hi", [P, KD, F], F16)
        w1_lo = sb("w1_lo", [P, KD, F], F16)
        w2_hi = sb("w2_hi", [P, FM, D], F16)
        w2_lo = sb("w2_lo", [P, FM, D], F16)
        y_b = sb("y_b", [P, 2, D])
        y_rows = [sb(f"y_rows{i}", [P, NS, D]) for i in range(2)]
        y_idx = [sb(f"y_idx{i}", [P, NS], I32) for i in range(2)]
        x1 = [sb(f"x1_{i}", [P, NJ, D]) for i in range(2)]
        a_st = sb("a_st", [P, NJ, 6])
        a_mv = sb("a_mv", [P, NJ, 2])
        a_rs = sb("a_rs", [P, NJ, 2])
        a_xn = sb("a_xn", [P, NJ, D])
        a_xT_hi = sb("a_xT_hi", [P, KD, SEQ], F16)
        a_xT_lo = sb("a_xT_lo", [P, KD, SEQ], F16)
        spare = arena
        assert FM * CAP >= (2 * KD + 3 * KD) * SEQ

        def in_spare(block, n):
            return spare[:, block * SEQ:(block + n) * SEQ].rearrange("p (k t) -> p k t", k=n)

        qk = w_raw[:, :, :, :].rearrange("p w m d -> p (w m d)").rearrange("p (k t) -> p k t", k=2 * KD)
        qk2 = in_spare(0, 2 * KD)
        kf = in_spare(2 * KD, KD)
        o_tok = in_spare(3 * KD, KD).rearrange("p k t -> p (k t)")
        oT_hi, oT_lo = [v.rearrange("p (k t) -> p k t", k=KD)
                        for v in half_precision(spare[:, 4 * KD * SEQ:5 * KD * SEQ])]
        xT_first = [v.rearrange("p (k t) -> p k t", k=KD) for v in half_precision(spare[:, 0:KD * SEQ])]

        spare_rows = rows_first[:, :, :, :].rearrange("p n j d -> p (n j d)")

        def in_rows(block):
            return spare_rows[:, block * NJ * D:(block + 1) * NJ * D]

        qf = [in_rows(i).rearrange("p (k t) -> p k t", k=KD) for i in range(2)]
        kt = [in_rows(2 + i).rearrange("p (j d) -> p j d", j=NJ) for i in range(2)]
        vt = [in_rows(4 + i).rearrange("p (j d) -> p j d", j=NJ) for i in range(2)]
        xb = [in_rows(6 + i).rearrange("p (j d) -> p j d", j=NJ) for i in range(2)]
        heads = D // HEAD_DIM
        zt = sb("zt", [P, NJ * heads])
        zr = [sb(f"zr{i}", [P, NJ * heads]) for i in range(2)]
        kv = sb("kv", [P, KD, P])

        ps = ctx.enter_context(nc.psum_tensor("ps", [P, 8, 512], F32))

        def feat_banks(b):
            return ps[:, b:b + 2, :]

        def tok_banks(b):
            return ps[:, b:b + 2, :].rearrange("p b (j d) -> p (b j) d", d=D)

        s_const = sem("s_const")
        s_zero = sem("s_zero")
        s_rzero = sem("s_rzero")
        s_wload = sem("s_wload")
        s_rload = sem("s_rload")
        s_bload = sem("s_bload")
        s_wg = sem("s_wg")
        s_fill = sem2("s_fill")
        s_base = sem("s_base")
        s_wT_pe = sem("s_wT_pe")
        s_wT = sem("s_wT")
        s_wTlo = sem("s_wTlo")
        s_wghi = sem("s_wghi")
        s_wglo = sem("s_wglo")
        s_rx = [sem(f"s_rx{n}") for n in range(NBAT)]
        s_x2 = sem("s_x2")
        s_rst = sem("s_rst")
        s_rvar = sem("s_rvar")
        s_rve = sem("s_rve")
        s_rsh = sem("s_rsh")
        s_rrs = sem("s_rrs")
        s_rid_first = sem("s_rid_first")
        s_rid = sem("s_rid")
        s_rxn = sem("s_rxn")
        s_rtp = sem("s_rtp")
        s_rxhi = sem("s_rxhi")
        s_rxlo = sem("s_rxlo")
        s_rlg = sem("s_rlg")
        s_rtop = sem("s_rtop")
        s_req = sem("s_req")
        s_rdl = sem("s_rdl")
        s_rsc = sem("s_rsc")
        s_rbest = sem("s_rbest")
        s_roh = sem("s_roh")
        s_rsumj = sem("s_rsumj")
        s_rseen = sem("s_rseen")
        s_rex = sem("s_rex")
        s_rsum = sem("s_rsum")
        s_rinv = sem("s_rinv")
        s_rgate = sem("s_rgate")
        s_rcnt = sem("s_rcnt")
        s_rpm = sem("s_rpm")
        s_rpos = sem("s_rpos")
        s_rslot = sem("s_rslot")
        s_rover = sem("s_rover")
        s_ridx = sem("s_ridx")
        s_rscat_first = sem("s_rscat_first")
        s_rscat = sem2("s_rscat")
        s_keep = sem2("s_keep")
        s_w1 = sem2("s_w1")
        s_w2 = sem2("s_w2")
        s_xe = sem2("s_xe")
        s_xs = sem("s_xs")
        s_yid = sem("s_yid")
        s_xtp = sem("s_xtp")
        s_xhi = sem("s_xhi")
        s_xlo = sem("s_xlo")
        s_w1hi = sem("s_w1hi")
        s_w1lo = sem("s_w1lo")
        s_w2hi = sem("s_w2hi")
        s_w2lo = sem("s_w2lo")
        s_h = sem("s_h")
        s_hf = sem("s_hf")
        s_hhi = sem("s_hhi")
        s_hlo = sem("s_hlo")
        s_y = sem("s_y")
        s_yb = sem("s_yb")
        s_yrow = sem("s_yrow")
        s_yscat = sem2("s_yscat")
        s_ax = sem2("s_ax")
        s_ast = sem("s_ast")
        s_avar = sem("s_avar")
        s_ave = sem("s_ave")
        s_ars = sem("s_ars")
        s_ash = sem("s_ash")
        s_axn = sem("s_axn")
        s_xb = sem("s_xb")
        s_atp = sem("s_atp")
        s_axhi = sem("s_axhi")
        s_axlo = sem("s_axlo")
        s_qkps = sem("s_qkps")
        s_qk = sem("s_qk")
        s_qk2 = sem("s_qk2")
        s_vps = sem("s_vps")
        s_v = sem("s_v")
        s_fps = sem("s_fps")
        s_f = sem("s_f")
        s_zps = sem("s_zps")
        s_zt = sem("s_zt")
        s_z = sem("s_z")
        s_ktps = sem("s_ktps")
        s_kt = sem("s_kt")
        s_kvps = sem("s_kvps")
        s_kv = sem("s_kv")
        s_ops = sem("s_ops")
        s_o = sem("s_o")
        s_otp = sem("s_otp")
        s_ohi = sem("s_ohi")
        s_olo = sem("s_olo")
        s_yps = sem("s_yps")

        s_aggr_go = sem("s_aggr_go")
        s_scatter_go = sem("s_scatter_go")

        s_split_go = sem("s_split_go")

        T_BANKS = [6, 7, 0]
        N_CONST = 13
        ALL_ROUTED = 16 * NJ * NBAT // 2
        ALL_SLOTS = 16 * NS * E // 2

        def steps(eng, first, loop_from, loop_to, last, body):
            for n in range(first, loop_from):
                body(n, n // 2, n)
            with eng.Fori(0, (loop_to - loop_from) // 2) as i:
                for u in range(2):
                    body(loop_from + u + 2 * i, (loop_from + u) // 2 + i, loop_from + u)
            for n in range(loop_to, last):
                body(n, n // 2, n)

        def route_rows(r):
            return rows_first[:, r, :, :] if r < NBAT else rows[r % 2]

        def route_mv(r):
            return mv_first[:, r, :, :] if r < NBAT else r_mv[r % 2]

        def route_xT(r):
            return xT_first if r < NBAT and r % 2 == 0 else [r_xT_hi[:, :, :], r_xT_lo[:, :, :]]

        def route_bank(r):
            return 0 if r < NBAT and r % 2 == 0 else 4

        def route_idx(r):
            return idx_first[:, r, :] if r < NBAT else r_idx[r % 2]

        block = ctx.enter_context(nc.Block())

        @block.sync
        def _(sp):
            def load_rows(n):
                sp.dma_start(rows_first[:, n, :, 0:D],
                             x_rows[n * SEQ:(n + 1) * SEQ, :].rearrange("(j p) d -> p j d", p=P)
                             ).then_inc(s_rx[n], 16)

            def fill(ph):
                sp.dma_start(routed[ph].rearrange("(n p) d -> p n d", p=P),
                             filler[:, :, :].to_broadcast([P, SLOTS // P, ROW])).then_inc(s_fill[ph], 16)

            def load_weights(n, h, r):
                e = n - (r // E) * E
                if r >= 2:
                    sp.wait_ge(s_w1lo, KD * (n - 1))
                sp.dma_start(w1_sb[r % 2][:, :, :],
                             w1[bass.ds(e, 1), :, :].rearrange("e (k p) f -> p (e k) f", p=P)
                             ).then_inc(s_w1[r % 2], 16)
                if r >= 2:
                    sp.wait_ge(s_w2lo, 2 * (n - 1))
                sp.dma_start(w2_sb[r % 2][:, :, :],
                             w2[bass.ds(e, 1), :, :].rearrange("e (m p) d -> p (e m) d", p=P)
                             ).then_inc(s_w2[r % 2], 16)

            def load_slots(n, h, r):
                ph = r // E
                if r >= 2:
                    sp.wait_ge(s_yrow, NS * (n - 1))
                    sp.wait_ge(s_yid, n - 1)
                sp.dma_start(xe[r % 2][:, :, :],
                             routed[ph][bass.ds((n - ph * E) * CAP, CAP), :].rearrange("(s p) d -> p s d", p=P)
                             ).then_inc(s_xe[r % 2], 16)

            def load_both(n, h, r):
                load_weights(n, h, r)
                load_slots(n, h, r)

            load_rows(0)
            load_rows(1)
            for i, w in enumerate((Wq, Wk, Wv, Wo)):
                sp.dma_start(w_raw[:, i, :, :], w.rearrange("(m p) d -> p m d", p=P)).then_inc(s_wload, 16)
            sp.dma_start(bias_rows[0:E * FM, :], b1.rearrange("e (m p) -> (e m) p", p=P)).then_inc(s_wload, 16)
            for i, b in enumerate((bq, bk)):
                lo = E * FM + i * KD
                sp.dma_start(bias_rows[lo:lo + KD, :], b.rearrange("(m p) -> m p", p=P)).then_inc(s_wload, 16)
            sp.dma_start(wg_sb[:, :, :], wg.rearrange("(k p) e -> p k e", p=P)).then_inc(s_wg, 16)
            for n in range(2, NBAT):
                load_rows(n)
            sp.wait_ge(s_const, N_CONST)
            fill(0)
            load_weights(0, 0, 0)
            load_weights(1, 0, 1)
            sp.dma_start(bv_sb[:, 0, :], bv.rearrange("(a d) -> a d", a=1).to_broadcast([P, D])).then_inc(s_bload, 16)
            sp.dma_start(bo_sb[:, 0, :], bo.rearrange("(a d) -> a d", a=1).to_broadcast([P, D])).then_inc(s_bload, 16)
            sp.dma_start(b2_sb[:, :, :].rearrange("p e d -> p (e d)"),
                         b2.rearrange("(a e) d -> a (e d)", a=1).to_broadcast([P, E * D])).then_inc(s_bload, 16)
            sp.wait_ge(s_rzero, 1)
            for hd in range(P // HEAD_DIM):
                at = slice(hd * HEAD_DIM, (hd + 1) * HEAD_DIM)
                sp.dma_start(r_heads[at, at], R).then_inc(s_rload, 16)
            sp.wait_ge(s_rscat_first, 16 * NJ * NBAT)
            load_slots(0, 0, 0)
            load_slots(1, 0, 1)
            sp.dma_start(x1_rows, x_rows).then_inc(s_base, 16)
            fill(1)
            steps(sp, 2, 2, E, E, load_both)

            def load_x1(n, h, r):
                if r >= 2:
                    sp.wait_ge(s_axn, n - 1)
                    sp.wait_ge(s_xb, n - 1)
                sp.dma_start(x1[r % 2][:, :, :],
                             x1_rows[bass.ds(n * SEQ, SEQ), :].rearrange("(j p) d -> p j d", p=P)
                             ).then_inc(s_ax[r % 2], 16)

            def store_x2(n, h, r):
                sp.wait_ge(s_x2, n + 1)
                sp.dma_start(out_rows[bass.ds(n * SEQ, SEQ), :].rearrange("(j p) d -> p j d", p=P),
                             rows[r % 2][:, :, 0:D]).then_inc(s_keep[r % 2], 16)

            for q in s_yscat:
                sp.wait_ge(q, ALL_SLOTS)
            load_x1(0, 0, 0)
            load_x1(1, 0, 1)
            load_weights(E, E // 2, E)
            load_weights(E + 1, E // 2, E + 1)

            def attention_traffic(n, h, r):
                load_x1(n, h, r)
                store_x2(n - 2, h - 1, r - 2)

            steps(sp, 2, 2, NBAT, NBAT, attention_traffic)
            store_x2(NBAT - 2, NBAT // 2 - 1, NBAT - 2)
            store_x2(NBAT - 1, NBAT // 2 - 1, NBAT - 1)
            for q in s_rscat:
                sp.wait_ge(q, ALL_ROUTED)
            load_slots(E, E // 2, E)
            load_slots(E + 1, E // 2, E + 1)
            steps(sp, E + 2, E + 2, 2 * E, 2 * E, load_both)
            for q in s_keep:
                sp.wait_ge(q, 16 * NBAT // 2)
            for q in s_yscat:
                sp.wait_ge(q, 2 * ALL_SLOTS)

        @block.gpsimd
        def _(pool):
            pool.memset(filler[:, :, :], 0.0).then_inc(s_const, 1)
            pool.memset(ident[:, :], 0.0).then_inc(s_const, 1)
            pool.memset(ones[:, :], 1.0).then_inc(s_const, 1)
            pool.memset(ones_b[:, :], 1.0).then_inc(s_const, 1)
            pool.memset(exponent[:, :], -0.5).then_inc(s_const, 1)
            pool.memset(eps[:, :], EPS_LN).then_inc(s_const, 1)
            pool.iota(rank_i[:, :], pattern=[[-1, E]], base=E, channel_multiplier=0).then_inc(s_const, 1)
            pool.iota(ids_i[:, :], pattern=[[P, T // P]], base=0, channel_multiplier=1).then_inc(s_const, 1)
            pool.wait_ge(s_const, 8)
            pool.memset(filler[:, :, ID:ID + 1], FAR).then_inc(s_const, 1)
            pool.affine_select(out=ident[:, :], in_=ident[:, :], compare_op=ALU.not_equal, fill=1.0,
                               base=0, pattern=[[-1, P]], channel_multiplier=1).then_inc(s_const, 1)
            pool.affine_select(out=upto[:, :], in_=ones_b[:, :], compare_op=ALU.is_ge, fill=0.0,
                               base=0, pattern=[[1, P]], channel_multiplier=-1).then_inc(s_const, 1)
            nh = P // HEAD_DIM
            pool.affine_select(out=minus_half_head[:, :], in_=ones[:, :], compare_op=ALU.is_ge, fill=0.0,
                               base=0, pattern=[[-HEAD_DIM, nh], [0, HEAD_DIM]],
                               channel_multiplier=1).then_inc(s_const, 1)
            pool.tensor_copy(ids[:, :], ids_i[:, :]).then_inc(s_const, 1)
            assert N_CONST == 13
            pool.wait_ge(s_const, N_CONST)
            pool.tensor_copy(rank[:, :], rank_i[:, :]).then_inc(s_const, 1)
            pool.affine_select(out=same_head[:, :], in_=minus_half_head[:, :], compare_op=ALU.is_ge, fill=0.0,
                               base=HEAD_DIM - 1, pattern=[[HEAD_DIM, nh], [0, HEAD_DIM]],
                               channel_multiplier=-1).then_inc(s_const, 1)
            pool.wait_ge(s_const, N_CONST + 2)
            pool.tensor_copy(head_cols[:, :],
                             same_head[:, :].rearrange("p (h d) -> p h d", d=HEAD_DIM)[:, :, 0]).then_inc(s_const, 1)
            pool.tensor_scalar(minus_half_head[:, :], same_head[:, :], -0.5, None, ALU.mult).then_inc(s_const, 1)

            def route_rstd(n, h, r):
                at = route_mv(r)[:, :, 1:2]
                pool.wait_ge(s_rvar, n + 1)
                pool.tensor_tensor(at, at, eps[:, :, None], ALU.add).then_inc(s_rve, 1)
                pool.wait_ge(s_rve, n + 1)
                pool.tensor_tensor(route_rows(r)[:, :, RSTD:RSTD + 1], at, exponent[:, :, None],
                                   ALU.pow).then_inc(s_rrs, 1)

            def route_scatter(n, h, r):
                ph = r // NBAT
                pool.wait_ge(s_fill[ph], 16)
                pool.wait_ge(s_ridx, n + 1)
                pool.wait_ge(s_rgate, n + 1)
                if r >= NBAT:
                    pool.wait_ge(s_rid, n - NBAT + 1)
                else:
                    pool.wait_ge(s_rid_first, 1)
                pool.wait_ge(s_rsh, n + 1)
                pool.sem_inc(s_scatter_go, 1)
                for j in range(NJ):
                    landed = s_rscat_first if ph == 0 else s_rscat[r % 2]
                    pool.indirect_dma_start(routed[ph], bass.IndirectOffsetOnAxis(ap=route_idx(r)[:, j:j + 1], axis=0),
                                            route_rows(r)[:, j, :], None, bounds_check=SLOTS - 1,
                                            oob_is_err=False).then_inc(landed, 16)

            for n in range(NBAT):
                route_rstd(n, n // 2, n)
            for n in range(NBAT):
                route_scatter(n, n // 2, n)

            def w2_high(n, h, r):
                pool.wait_ge(s_w2[r % 2], 16 * (h + 1))
                if r >= 1:
                    pool.wait_ge(s_y, NS * n)
                pool.sem_inc(s_split_go, 1)
                for i in range(2):
                    nc.gpsimd.tensor_scalar(w2_hi[:, i * FM // 2:(i + 1) * FM // 2, :],
                                            w2_sb[r % 2][:, i * FM // 2:(i + 1) * FM // 2, :],
                                            W_SCALE, None, ALU.mult).then_inc(s_w2hi, 1)

            def slots_out(n, h, r):
                ph = r // E
                pool.wait_ge(s_yid, n + 1)
                for s in range(NS):
                    pool.wait_ge(s_yrow, NS * n + s + 1)
                    pool.sem_inc(s_scatter_go, 1)
                    pool.indirect_dma_start(after_ffn[ph],
                                            bass.IndirectOffsetOnAxis(ap=y_idx[r % 2][:, s:s + 1], axis=0),
                                            y_rows[r % 2][:, s, :], None, bounds_check=T - 1,
                                            oob_is_err=False).then_inc(s_yscat[r % 2], 16)
                if r % E != E - 1:
                    w2_high(n + 1, h if r % 2 == 0 else h + 1, r + 1)

            w2_high(0, 0, 0)
            pool.wait_ge(s_base, 16)
            steps(pool, 0, 0, E - 2, E, slots_out)

            def add_bo(n, h, r):
                pool.wait_ge(s_ax[r % 2], 16 * (h + 1))
                if r >= 2:
                    pool.wait_ge(s_x2, n - 1)
                pool.tensor_tensor(xb[r % 2][:, :, :], x1[r % 2][:, :, :],
                                   bo_sb[:, :, :].to_broadcast([P, NJ, D]), ALU.add).then_inc(s_xb, 1)

            def norm_rstd(n, h, r):
                at = a_mv[:, :, 1:2]
                pool.wait_ge(s_avar, n + 1)
                pool.tensor_tensor(at, at, eps[:, :, None], ALU.add).then_inc(s_ave, 1)
                pool.wait_ge(s_ave, n + 1)
                if r >= 1:
                    pool.wait_ge(s_axn, n)
                pool.tensor_tensor(a_rs[:, :, 1:2], at, exponent[:, :, None], ALU.pow).then_inc(s_ars, 1)

            def attend(n, h, r):
                hb = h - 1 if r % 2 == 0 else h
                if r < NBAT:
                    add_bo(n, h, r)
                if r < NBAT - 1:
                    norm_rstd(n + 1, h, r + 1)
                if r >= 1:
                    route_rstd(NBAT + n - 1, NBAT // 2 + hb, NBAT + r - 1)
                if r >= 1:
                    route_scatter(NBAT + n - 1, NBAT // 2 + hb, NBAT + r - 1)

            pool.wait_ge(s_bload, 48)
            norm_rstd(0, 0, 0)
            steps(pool, 0, 3, NBAT - 1, NBAT + 1, attend)
            w2_high(E, E // 2, E)
            for q in s_keep:
                pool.wait_ge(q, 16 * NBAT // 2)
            steps(pool, E, E, 2 * E - 2, 2 * E, slots_out)

        @block.scalar
        def _(act):
            for i in range(4):
                act.wait_ge(s_wT_pe, i + 1)
                nc.scalar.activation(wT_hi[:, i, :, :].rearrange("p k d -> p (k d)"), ps[:, i, :], ACT.Copy,
                                     scale=W_SCALE).then_inc(s_wT, 1)
            act.wait_ge(s_wT_pe, 5)
            nc.scalar.mul(b1_cols[:, :], ps[:, 4, 0:E * FM], H_SCALE).then_inc(s_wT, 1)
            nc.scalar.mul(qk_bias[:, :], ps[:, 4, E * FM:E * FM + 2 * KD], QSCALE).then_inc(s_wT, 1)

            def route_norm(n, h, r):
                at = route_rows(r)
                act.wait_ge(s_rsh, n + 1)
                if r >= 2:
                    act.wait_ge(s_rtp, n - 1)
                for j in range(NJ):
                    ins = nc.scalar.activation(r_xn[r % 2][:, j, :], at[:, j, 0:D], ACT.Identity,
                                               scale=at[:, j, RSTD:RSTD + 1], bias=at[:, j, SHIFT:SHIFT + 1])
                ins.then_inc(s_rxn, 1)

            def route_evacuate(n, h, r):
                act.wait_ge(s_rtp, n + 1)
                if r >= NBAT:
                    act.wait_ge(s_rlg, n)
                elif r >= 2:
                    act.wait_ge(s_rlg, n - 1)
                nc.scalar.copy(route_xT(r)[0], feat_banks(route_bank(r))).then_inc(s_rxhi, 1)

            def route_exp(n, h, r):
                act.wait_ge(s_rdl, n + 1)
                if r >= 1:
                    act.wait_ge(s_rsum, n)
                nc.scalar.activation(r_ex[:, :, :], r_dl[:, :, :], ACT.Exp,
                                     scale=1.0 / W_SCALE).then_inc(s_rex, 1)

            route_norm(0, 0, 0)
            route_norm(1, 0, 1)
            route_evacuate(0, 0, 0)
            for n in range(NBAT):
                if n + 1 < NBAT:
                    route_evacuate(n + 1, (n + 1) // 2, n + 1)
                if n + 2 < NBAT:
                    route_norm(n + 2, (n + 2) // 2, n + 2)
                route_exp(n, n // 2, n)

            def slots_T(n, h, r):
                for c in range((NS + 1) // 2):
                    w = min(2, NS - 2 * c) * P
                    act.wait_ge(s_xtp, 3 * n + c + 1)
                    nc.scalar.copy(xT_hi[:, :, 2 * c * P:2 * c * P + w],
                                   ps[:, T_BANKS[c], :].rearrange("p (k t) -> p k t", k=KD)[:, :, 0:w]
                                   ).then_inc(s_xhi, 1)

            def w1_high(n, h, r):
                act.wait_ge(s_w1[r % 2], 16 * (h + 1))
                if r >= 1:
                    act.wait_ge(s_h, FM * n)
                for k in range(KD):
                    nc.scalar.activation(w1_hi[:, k, :], w1_sb[r % 2][:, k, :], ACT.Copy,
                                         scale=W_SCALE).then_inc(s_w1hi, 1)

            def relu(n, h, r):
                if r >= 1:
                    act.wait_ge(s_y, NS * n)
                for m in range(FM):
                    act.wait_ge(s_h, FM * n + m + 1)
                    if r >= 1 or m >= 2:
                        act.wait_ge(s_hlo, FM * n + m - 1)
                    b = 2 * (m % 2)
                    for dst, done in ((h_full[:, m % 2, :], s_hf), (hT_hi[:, m, :], s_hhi)):
                        nc.scalar.activation(dst.rearrange("p (a t) -> p a t", a=2), ps[:, b:b + 2, 0:HALF],
                                             ACT.Relu, scale=H_SCALE / W_SCALE,
                                             bias=b1_cols[:, bass.ds((n - (r // E) * E) * FM + m, 1)]
                                             ).then_inc(done, 1)

            def expert(n, h, r):
                relu(n, h, r)
                if r % E != E - 1:
                    slots_T(n + 1, h, r + 1)
                    w1_high(n + 1, h if r % 2 == 0 else h + 1, r + 1)

            w1_high(0, 0, 0)
            slots_T(0, 0, 0)
            steps(act, 0, 2, E - 2, E, expert)

            def norm(n, h, r):
                act.wait_ge(s_ash, n + 1)
                if r >= 1:
                    act.wait_ge(s_atp, n)
                for j in range(NJ):
                    ins = nc.scalar.activation(a_xn[:, j, :], x1[r % 2][:, j, :], ACT.Identity,
                                               scale=a_rs[:, j, 1:2], bias=a_rs[:, j, 0:1])
                ins.then_inc(s_axn, 1)

            def attend(n, h, r):
                early, late = r < NBAT, r >= 1
                if early:
                    act.wait_ge(s_atp, n + 1)
                    if r >= 1:
                        act.wait_ge(s_vps, n)
                    nc.scalar.copy(a_xT_hi[:, :, :], feat_banks(0)).then_inc(s_axhi, 1)
                if late:
                    act.wait_ge(s_otp, n)
                    if r >= 2:
                        act.wait_ge(s_yps, n - 1)
                    nc.scalar.copy(oT_hi, feat_banks(0)).then_inc(s_ohi, 1)
                if early:
                    for c in range(2 * KD):
                        act.wait_ge(s_qk, 2 * KD * n + c + 1)
                        if c == 0 and r >= 1:
                            act.wait_ge(s_fps, 2 * KD * n)
                        nc.scalar.activation(qk2[:, c, :], qk[:, c, :], ACT.Square).then_inc(s_qk2, 1)
                if r < NBAT - 1:
                    norm(n + 1, h, r + 1)
                if early:
                    for c in range(2 * KD):
                        act.wait_ge(s_fps, 2 * KD * n + c + 1)
                        if c == 0 and r >= 2:
                            act.wait_ge(s_ops, n - 1)
                        if c == KD and r >= 1:
                            act.wait_ge(s_ktps, n)
                        dst = qf[r % 2][:, c, :] if c < KD else kf[:, c - KD, :]
                        nc.scalar.activation(dst, ps[:, 4 + c, :], ACT.Exp).then_inc(s_f, 1)
                if late:
                    route_norm(NBAT + n - 1, h, NBAT + r - 1)
                    route_evacuate(NBAT + n - 1, h, NBAT + r - 1)
                if early:
                    act.wait_ge(s_ktps, n + 1)
                    if r >= 2:
                        act.wait_ge(s_kvps, n - 1)
                    nc.scalar.copy(kt[r % 2][:, :, :], tok_banks(6)).then_inc(s_kt, 1)
                if late:
                    route_exp(NBAT + n - 1, h, NBAT + r - 1)

            norm(0, 0, 0)
            steps(act, 0, 3, NBAT - 1, NBAT + 1, attend)
            w1_high(E, E // 2, E)
            slots_T(E, E // 2, E)
            steps(act, E, E, 2 * E - 2, 2 * E, expert)

        @block.tensor
        def _(pe):
            pe.wait_ge(s_const, N_CONST)
            pe.wait_ge(s_wload, 16 * 7)
            for i in range(4):
                for k in range(KD):
                    for m in range(KD):
                        mm = nc.tensor.transpose(ps[:, i, k * D + m * P:k * D + (m + 1) * P],
                                                 w_raw[:, i, m, k * P:(k + 1) * P], ident[:, :])
                mm.then_inc(s_wT_pe, 1)
            nb = E * FM + 2 * KD
            nc.tensor.transpose(ps[:, 4, 0:nb], bias_rows[:, :], ident[0:nb, 0:nb]).then_inc(s_wT_pe, 1)
            pe.wait_ge(s_wT, 6)
            pe.wait_ge(s_wTlo, 4)
            pe.wait_ge(s_wglo, 1)

            def product(dst, pairs):
                for i, (stationary, moving) in enumerate(pairs):
                    mm = nc.tensor.matmul(dst, stationary, moving, start=(i == 0), stop=(i == len(pairs) - 1))
                return mm

            def rows_T(n, h, r):
                b = route_bank(r)
                pe.wait_ge(s_rxn, n + 1)
                if r > NBAT:
                    pe.wait_ge(s_rxlo, n)
                elif 2 <= r < NBAT:
                    pe.wait_ge(s_rxlo, n - 1)
                for j in range(NJ):
                    for k in range(KD):
                        mm = nc.tensor.transpose(ps[:, b + k, j * P:(j + 1) * P],
                                                 r_xn[r % 2][:, j, k * P:(k + 1) * P], ident[:, :])
                mm.then_inc(s_rtp, 1)

            def logits(n, h, r):
                pe.wait_ge(s_rxlo, n + 1)
                if r >= 1:
                    pe.wait_ge(s_rdl, n)
                    pe.wait_ge(s_req, n)
                x_hi, x_lo = route_xT(r)
                for j in range(NJ):
                    mm = product(ps[:, 3, j * E:(j + 1) * E],
                                 [(x[:, k, j * P:(j + 1) * P], w[:, k, :]) for k in range(KD)
                                  for x, w in ((x_hi, wg_hi), (x_hi, wg_lo), (x_lo, wg_hi), (x_lo, wg_lo))])
                mm.then_inc(s_rlg, 1)

            def counts(n, h, r):
                pe.wait_ge(s_roh, n + 1)
                if r % NBAT == 0:
                    pe.wait_ge(s_zero, r // NBAT + 1)
                else:
                    pe.wait_ge(s_rseen, n - r // NBAT)
                if r >= 1:
                    pe.wait_ge(s_rpm, n)
                oh = r_oh[r % 2]
                dst = ps[:, 2, 0:NJ * E].rearrange("p (j e) -> p j e", e=E)
                nc.tensor.matmul(dst, upto[:, :], oh[:, :, :], start=True, stop=False)
                nc.tensor.matmul(dst, ones_b[:, :], r_seen[r % 2][:, :, :].to_broadcast([P, NJ, E]),
                                 start=False, stop=False)
                for back in range(1, NJ):
                    mm = nc.tensor.matmul(dst[:, back:NJ, :], ones_b[:, :], oh[:, 0:NJ - back, :],
                                          start=False, stop=(back == NJ - 1))
                mm.then_inc(s_rcnt, 1)

            rows_T(0, 0, 0)
            for n in range(NBAT + 1):
                if n + 1 < NBAT:
                    rows_T(n + 1, (n + 1) // 2, n + 1)
                if n < NBAT:
                    logits(n, n // 2, n)
                if n >= 1:
                    counts(n - 1, (n - 1) // 2, n - 1)

            def slots_T(n, h, r):
                pe.wait_ge(s_xs, n + 1)
                for c in range((NS + 1) // 2):
                    if c == 2 and r % E:
                        pe.wait_ge(s_hhi, FM * n - 1)
                    for s in range(2 * c, min(2 * c + 2, NS)):
                        for k in range(KD):
                            at = k * 2 * P + (s - 2 * c) * P
                            mm = nc.tensor.transpose(ps[:, T_BANKS[c], at:at + P],
                                                     xs[:, s, k * P:(k + 1) * P], ident[:, :])
                    mm.then_inc(s_xtp, 1)

            def hidden(n, h, r):
                pe.wait_ge(s_xlo, 3 * n + 3)
                pe.wait_ge(s_w1lo, KD * (n + 1))
                for m in range(FM):
                    if r >= 1 or m >= 2:
                        pe.wait_ge(s_hhi, FM * n + m - 1)
                    b = 2 * (m % 2)
                    parts = [(w1_hi, xT_hi), (w1_hi, xT_lo), (w1_lo, xT_hi)]
                    for k in range(KD):
                        for i, (w_part, x_part) in enumerate(parts):
                            for a in range(2):
                                mm = nc.tensor.matmul(ps[:, b + a, 0:HALF], w_part[:, k, m * P:(m + 1) * P],
                                                      x_part[:, k, a * HALF:(a + 1) * HALF],
                                                      start=(k == 0 and i == 0), stop=(k == KD - 1 and i == 2))
                    mm.then_inc(s_h, 1)

            def expert_out(n, h, r):
                pe.wait_ge(s_hlo, FM * (n + 1))
                pe.wait_ge(s_w2lo, 2 * (n + 1))
                for s in range(NS):
                    if r >= 1 or s >= 2:
                        pe.wait_ge(s_yb, NS * n + s - 1)
                    b = 4 + s % 2 if r % 2 == 0 else 4 + (s + 1) % 2
                    parts = [(hT_hi, w2_hi), (hT_hi, w2_lo), (hT_lo, w2_hi)]
                    for m in range(FM):
                        for i, (h_part, w_part) in enumerate(parts):
                            mm = nc.tensor.matmul(ps[:, b, 0:D], h_part[:, m, s * P:(s + 1) * P], w_part[:, m, :],
                                                  start=(m == 0 and i == 0), stop=(m == FM - 1 and i == 2))
                    mm.then_inc(s_y, 1)

            def expert(n, h, r):
                hidden(n, h, r)
                if r % E != E - 1:
                    slots_T(n + 1, h, r + 1)
                expert_out(n, h, r)

            slots_T(0, 0, 0)
            steps(pe, 0, 2, E - 2, E, expert)

            def attend(n, h, r):
                early, late = r < NBAT, r >= 1
                b, rb = n - 1, r - 1
                if early:
                    pe.wait_ge(s_axn, n + 1)
                    if r >= 1:
                        pe.wait_ge(s_zt, n)
                    if r >= 2:
                        pe.wait_ge(s_x2, n - 1)
                    for j in range(NJ):
                        for k in range(KD):
                            mm = nc.tensor.transpose(ps[:, k, j * P:(j + 1) * P],
                                                     a_xn[:, j, k * P:(k + 1) * P], ident[:, :])
                    mm.then_inc(s_atp, 1)
                if late:
                    pe.wait_ge(s_kt, b + 1)
                    pe.wait_ge(s_v, b + 1)
                    if rb >= 1:
                        pe.wait_ge(s_rdl, NBAT + b)
                        pe.wait_ge(s_req, NBAT + b)
                    for m in range(KD):
                        mm = product(ps[:, 3, m * P:(m + 1) * P],
                                     [(kt[rb % 2][:, j, m * P:(m + 1) * P], vt[rb % 2][:, j, m * P:(m + 1) * P])
                                      for j in range(NJ)])
                    mm.then_inc(s_kvps, 1)
                    pe.wait_ge(s_kv, b + 1)
                    if rb >= 1:
                        pe.wait_ge(s_rpm, NBAT + b)
                    for j in range(NJ):
                        for m in range(KD):
                            mm = nc.tensor.matmul(tok_banks(2)[:, j, m * P:(m + 1) * P],
                                                  qf[rb % 2][:, m, j * P:(j + 1) * P], kv[:, m, :],
                                                  start=True, stop=True)
                    mm.then_inc(s_ops, 1)
                if early:
                    pe.wait_ge(s_axlo, n + 1)
                    if r >= 1:
                        pe.wait_ge(s_kt, n)
                    if r >= 2:
                        pe.wait_ge(s_rxlo, NBAT + n - 1)
                    for c in range(2 * KD):
                        w, m = c // KD, c % KD
                        product(ps[:, 4 + c, :],
                                [(w_part[:, w, k, m * P:(m + 1) * P], x_part[:, k, :]) for k in range(KD)
                                 for w_part, x_part in ((wT_hi, a_xT_hi), (wT_hi, a_xT_lo), (wT_lo, a_xT_hi))]
                                ).then_inc(s_qkps, 1)
                if late:
                    pe.wait_ge(s_o, b + 1)
                    for j in range(NJ):
                        for k in range(KD):
                            mm = nc.tensor.transpose(ps[:, k, j * P:(j + 1) * P],
                                                     o_tok[:, j * D + k * P:j * D + (k + 1) * P], ident[:, :])
                    mm.then_inc(s_otp, 1)
                if early:
                    if r >= 1:
                        pe.wait_ge(s_o, b + 1)
                    for j in range(NJ):
                        mm = product(tok_banks(2)[:, j, :],
                                     [(x_part[:, k, j * P:(j + 1) * P], w_part[:, 2, k, :]) for k in range(KD)
                                      for x_part, w_part in ((a_xT_hi, wT_hi), (a_xT_hi, wT_lo), (a_xT_lo, wT_hi))])
                    mm.then_inc(s_vps, 1)
                if late:
                    pe.wait_ge(s_olo, b + 1)
                    for j in range(NJ):
                        mm = product(tok_banks(0)[:, j, :],
                                     [(o_part[:, m, j * P:(j + 1) * P], w_part[:, 3, m, :]) for m in range(KD)
                                      for o_part, w_part in ((oT_hi, wT_hi), (oT_hi, wT_lo), (oT_lo, wT_hi))])
                    mm.then_inc(s_yps, 1)
                if early:
                    for c in range(2 * KD):
                        pe.wait_ge(s_qk, 2 * KD * n + c + 1)
                        nc.tensor.matmul(ps[:, 4 + c, :], r_heads[:, :], qk[:, c, :], start=True, stop=False)
                        pe.wait_ge(s_qk2, 2 * KD * n + c + 1)
                        nc.tensor.matmul(ps[:, 4 + c, :], minus_half_head[:, :], qk2[:, c, :],
                                         start=False, stop=True).then_inc(s_fps, 1)
                if early:
                    pe.wait_ge(s_f, 2 * KD * (n + 1))
                    for j in range(NJ):
                        for m in range(KD):
                            mm = nc.tensor.transpose(tok_banks(6)[:, j, m * P:(m + 1) * P],
                                                     kf[:, m, j * P:(j + 1) * P], ident[:, :])
                    mm.then_inc(s_ktps, 1)
                if late:
                    rows_T(NBAT + b, h, NBAT + rb)
                if early:
                    if late:
                        pe.wait_ge(s_x2, b + 1)
                    for j in range(NJ):
                        for m in range(KD):
                            at = j * heads + m * (P // HEAD_DIM)
                            mm = nc.tensor.matmul(ps[:, 0, at:at + P // HEAD_DIM], qf[r % 2][:, m, j * P:(j + 1) * P],
                                                  head_cols[:, :], start=True, stop=True)
                    mm.then_inc(s_zps, 1)
                if late:
                    if early:
                        pe.wait_ge(s_v, n + 1)
                    logits(NBAT + b, h, NBAT + rb)
                    counts(NBAT + b, h, NBAT + rb)

            pe.wait_ge(s_const, N_CONST + 4)
            pe.wait_ge(s_rload, 16 * (P // HEAD_DIM))
            steps(pe, 0, 3, NBAT - 1, NBAT + 1, attend)
            slots_T(E, E // 2, E)
            steps(pe, E, E, 2 * E - 2, 2 * E, expert)

        @block.vector
        def _(dve):
            dve.memset(r_heads[:, :], 0.0).then_inc(s_rzero, 1)
            dve.memset(r_seen[0][:, 0, :], 0.0).then_inc(s_zero, 1)
            dve.wait_ge(s_const, N_CONST + 1)
            nc.vector.tensor_copy(rows_first[:, :, :, ID].rearrange("p n j -> p n j"),
                                  ids[:, :].rearrange("p (n j) -> p n j", j=NJ)).then_inc(s_rid_first, 1)

            def route_stats(n, h, r):
                x_at = route_rows(r)
                if r < NBAT:
                    dve.wait_ge(s_rx[r], 16)
                else:
                    dve.wait_ge(s_x2, n - NBAT + 1)
                for j in range(NJ):
                    ins = nc.vector.bn_stats(r_st[r % 2][:, j, :], x_at[:, j, 0:D])
                ins.then_inc(s_rst, 1)
                if r >= NBAT:
                    nc.vector.tensor_copy(x_at[:, :, ID:ID + 1],
                                          ids[:, bass.ds((n - NBAT) * NJ, NJ)][:, :, None]).then_inc(s_rid, 1)
                dve.wait_ge(s_rst, n + 1)
                if r > NBAT:
                    dve.wait_ge(s_rrs, n)
                dve.sem_inc(s_aggr_go, 1)
                for j in range(NJ):
                    ins = nc.vector.bn_aggr(route_mv(r)[:, j, :], r_st[r % 2][:, j, :])
                ins.then_inc(s_rvar, 1)

            def route_low(n, h, r):
                hi, lo = route_xT(r)
                dve.wait_ge(s_rxhi, n + 1)
                nc.vector.tensor_tensor(lo, feat_banks(route_bank(r)), hi, ALU.subtract).then_inc(s_rxlo, 1)

            def route_shift(n, h, r):
                x_at = route_rows(r)
                dve.wait_ge(s_rrs, n + 1)
                nc.vector.scalar_tensor_tensor(out=x_at[:, :, SHIFT:SHIFT + 1], in0=route_mv(r)[:, :, 0:1],
                                               scalar=-1.0, in1=x_at[:, :, RSTD:RSTD + 1],
                                               op0=ALU.mult, op1=ALU.mult).then_inc(s_rsh, 1)

            def route_choose(n, h, r):
                lg = ps[:, 3, 0:NJ * E].rearrange("p (j e) -> p j e", e=E)
                wide = [P, NJ, E]
                oh, seen, nxt, best = r_oh[r % 2], r_seen[r % 2], r_seen[1 - r % 2], r_best[r % 2]
                dve.wait_ge(s_rlg, n + 1)
                nc.vector.tensor_reduce(r_top[:, :], lg, AX.X, ALU.max).then_inc(s_rtop, 1)
                dve.wait_ge(s_rtop, n + 1)
                nc.vector.tensor_tensor(r_eq[:, :, :], lg, r_top[:, :, None].to_broadcast(wide),
                                        ALU.is_ge).then_inc(s_req, 1)
                if r >= 1:
                    dve.wait_ge(s_rex, n)
                nc.vector.tensor_tensor(r_dl[:, :, :], lg, r_top[:, :, None].to_broadcast(wide),
                                        ALU.subtract).then_inc(s_rdl, 1)
                dve.wait_ge(s_req, n + 1)
                nc.vector.tensor_tensor(r_sc[:, :, :], r_eq[:, :, :], rank[:, None, :].to_broadcast(wide),
                                        ALU.mult).then_inc(s_rsc, 1)
                dve.wait_ge(s_rsc, n + 1)
                nc.vector.tensor_reduce(best[:, :], r_sc[:, :, :], AX.X, ALU.max).then_inc(s_rbest, 1)
                dve.wait_ge(s_rbest, n + 1)
                if r >= 2:
                    dve.wait_ge(s_rcnt, n - 1)
                nc.vector.tensor_tensor(oh[:, :, :], r_sc[:, :, :], best[:, :, None].to_broadcast(wide),
                                        ALU.is_equal).then_inc(s_roh, 1)

            def route_seen(n, h, r):
                oh, seen, nxt = r_oh[r % 2], r_seen[r % 2], r_seen[1 - r % 2]
                if r % NBAT == NBAT - 1:
                    return
                dve.wait_ge(s_roh, n + 1)
                with nc.allow_low_precision(reason="counts up to 4, exact in bfloat16"):
                    nc.vector.tensor_reduce(r_sumj[:, :], oh[:, :, :].rearrange("p j e -> p e j"), AX.X,
                                            ALU.add).then_inc(s_rsumj, 1)
                skipped = r // NBAT
                dve.wait_ge(s_rsumj, n + 1 - skipped)
                if r >= 1:
                    dve.wait_ge(s_rcnt, n)
                if r % NBAT == 0:
                    dve.wait_ge(s_zero, r // NBAT + 1)
                nc.vector.tensor_tensor(nxt[:, 0, :], seen[:, 0, :], r_sumj[:, :], ALU.add).then_inc(s_rseen, 1)

            def route_place(n, h, r):
                x_at = route_rows(r)
                dve.wait_ge(s_rex, n + 1)
                nc.vector.tensor_reduce(r_sum[:, :], r_ex[:, :, :], AX.X, ALU.add).then_inc(s_rsum, 1)
                dve.wait_ge(s_rsum, n + 1)
                nc.vector.reciprocal(r_inv[:, :], r_sum[:, :]).then_inc(s_rinv, 1)
                dve.wait_ge(s_rcnt, n + 1)
                nc.vector.tensor_tensor(r_pm[:, :, :], r_oh[r % 2][:, :, :],
                                        ps[:, 2, 0:NJ * E].rearrange("p (j e) -> p j e", e=E),
                                        ALU.mult).then_inc(s_rpm, 1)
                dve.wait_ge(s_rinv, n + 1)
                nc.vector.tensor_scalar(x_at[:, :, GT:GT + 1], r_inv[:, :, None], 0.5, None,
                                        ALU.mult).then_inc(s_rgate, 1)
                dve.wait_ge(s_rpm, n + 1)
                nc.vector.tensor_reduce(r_pos[:, :], r_pm[:, :, :], AX.X, ALU.add).then_inc(s_rpos, 1)
                dve.wait_ge(s_rpos, n + 1)
                nc.vector.scalar_tensor_tensor(out=r_slot[:, :], in0=r_best[r % 2][:, :], scalar=-float(CAP),
                                               in1=r_pos[:, :], op0=ALU.mult, op1=ALU.add).then_inc(s_rslot, 1)
                nc.vector.tensor_scalar(r_over[:, :], r_pos[:, :], float(CAP), FAR, ALU.is_gt,
                                        ALU.mult).then_inc(s_rover, 1)
                dve.wait_ge(s_rslot, n + 1)
                dve.wait_ge(s_rover, n + 1)
                nc.vector.scalar_tensor_tensor(out=route_idx(r)[:, :], in0=r_slot[:, :], scalar=float(SLOTS - 1),
                                               in1=r_over[:, :], op0=ALU.add, op1=ALU.add).then_inc(s_ridx, 1)

            def projections_low():
                for i in range(4):
                    dve.wait_ge(s_wT, i + 1)
                    nc.vector.scalar_tensor_tensor(out=wT_lo[:, i, :, :].rearrange("p k d -> p (k d)"),
                                                   in0=ps[:, i, :], scalar=W_SCALE,
                                                   in1=wT_hi[:, i, :, :].rearrange("p k d -> p (k d)"),
                                                   op0=ALU.mult, op1=ALU.subtract).then_inc(s_wTlo, 1)
                dve.wait_ge(s_wg, 16)
                nc.vector.tensor_scalar(wg_hi[:, :, :], wg_sb[:, :, :], W_SCALE, None, ALU.mult).then_inc(s_wghi, 1)
                dve.wait_ge(s_wghi, 1)
                nc.vector.scalar_tensor_tensor(out=wg_lo[:, :, :], in0=wg_sb[:, :, :], scalar=W_SCALE,
                                               in1=wg_hi[:, :, :], op0=ALU.mult, op1=ALU.subtract).then_inc(s_wglo, 1)

            for n in range(NBAT + 1):
                if n == 2:
                    projections_low()
                if n < NBAT:
                    route_stats(n, n // 2, n)
                if n >= 1:
                    route_shift(n - 1, (n - 1) // 2, n - 1)
            route_low(0, 0, 0)
            for n in range(NBAT + 1):
                if n + 1 < NBAT:
                    route_low(n + 1, (n + 1) // 2, n + 1)
                if n < NBAT:
                    route_choose(n, n // 2, n)
                    route_seen(n, n // 2, n)
                if n >= 1:
                    route_place(n - 1, (n - 1) // 2, n - 1)

            def slots_norm(n, h, r):
                at = xe[r % 2]
                dve.wait_ge(s_xe[r % 2], 16 * (h + 1))
                if r >= 1:
                    dve.wait_ge(s_xtp, 3 * n)
                for s in range(NS):
                    ins = nc.vector.tensor_scalar(xs[:, s, :], at[:, s, 0:D], at[:, s, RSTD:RSTD + 1],
                                                  at[:, s, SHIFT:SHIFT + 1], ALU.mult, ALU.add)
                ins.then_inc(s_xs, 1)
                if r >= 2:
                    dve.wait_ge(s_yscat[r % 2], 16 * NS * h)
                nc.vector.tensor_copy(y_idx[r % 2][:, :, None], at[:, :, ID:ID + 1]).then_inc(s_yid, 1)

            def w1_low(n, h, r):
                for k in range(KD):
                    dve.wait_ge(s_w1hi, KD * n + k + 1)
                    nc.vector.scalar_tensor_tensor(out=w1_lo[:, k, :], in0=w1_sb[r % 2][:, k, :], scalar=W_SCALE,
                                                   in1=w1_hi[:, k, :], op0=ALU.mult,
                                                   op1=ALU.subtract).then_inc(s_w1lo, 1)

            def w2_low(n, h, r, i):
                at = slice(i * FM // 2, (i + 1) * FM // 2)
                dve.wait_ge(s_w2hi, 2 * n + i + 1)
                nc.vector.scalar_tensor_tensor(out=w2_lo[:, at, :], in0=w2_sb[r % 2][:, at, :], scalar=W_SCALE,
                                               in1=w2_hi[:, at, :], op0=ALU.mult,
                                               op1=ALU.subtract).then_inc(s_w2lo, 1)

            def slots_T_low(n, h, r):
                for c in range((NS + 1) // 2):
                    w = min(2, NS - 2 * c) * P
                    dve.wait_ge(s_xhi, 3 * n + c + 1)
                    nc.vector.tensor_tensor(xT_lo[:, :, 2 * c * P:2 * c * P + w],
                                            ps[:, T_BANKS[c], :].rearrange("p (k t) -> p k t", k=KD)[:, :, 0:w],
                                            xT_hi[:, :, 2 * c * P:2 * c * P + w], ALU.subtract).then_inc(s_xlo, 1)

            def h_low(n, h, r, m):
                dve.wait_ge(s_hhi, FM * n + m + 1)
                nc.vector.tensor_tensor(hT_lo[:, m, :], h_full[:, m % 2, :], hT_hi[:, m, :],
                                        ALU.subtract).then_inc(s_hlo, 1)

            def slots_add(n, h, r):
                at = xe[r % 2]
                for s in range(NS):
                    q = s % 2 if r % 2 == 0 else (s + 1) % 2
                    dve.wait_ge(s_y, NS * n + s + 1)
                    if r >= 1 or s >= 2:
                        dve.wait_ge(s_yrow, NS * n + s - 1)
                    nc.vector.scalar_tensor_tensor(out=y_b[:, q, :], in0=ps[:, 4 + q, 0:D],
                                                   scalar=1.0 / (H_SCALE * W_SCALE),
                                                   in1=b2_sb[:, bass.ds(n - (r // E) * E, 1), :].rearrange(
                                                       "p e d -> p (e d)"),
                                                   op0=ALU.mult, op1=ALU.add).then_inc(s_yb, 1)
                    dve.wait_ge(s_yb, NS * n + s + 1)
                    nc.vector.scalar_tensor_tensor(out=y_rows[r % 2][:, s, :], in0=y_b[:, q, :],
                                                   scalar=at[:, s, GT:GT + 1], in1=at[:, s, 0:D],
                                                   op0=ALU.mult, op1=ALU.add).then_inc(s_yrow, 1)

            def expert(n, h, r):
                hn = h if r % 2 == 0 else h + 1
                for m in range(FM):
                    h_low(n, h, r, m)
                    if m in (FM // 2, FM // 2 + 2):
                        w2_low(n, h, r, m // 2 - FM // 4)
                    if m == FM // 2 - 1 and r % E != E - 1:
                        slots_norm(n + 1, hn, r + 1)
                if r % E != E - 1:
                    slots_T_low(n + 1, hn, r + 1)
                    w1_low(n + 1, hn, r + 1)
                slots_add(n, h, r)

            dve.wait_ge(s_bload, 48)
            w1_low(0, 0, 0)
            slots_norm(0, 0, 0)
            slots_T_low(0, 0, 0)
            steps(dve, 0, 2, E - 2, E, expert)

            def norm_stats(n, h, r):
                dve.wait_ge(s_ax[r % 2], 16 * (h + 1))
                for j in range(NJ):
                    ins = nc.vector.bn_stats(a_st[:, j, :], x1[r % 2][:, j, :])
                ins.then_inc(s_ast, 1)
                dve.wait_ge(s_ast, n + 1)
                dve.sem_inc(s_aggr_go, 1)
                for j in range(NJ):
                    ins = nc.vector.bn_aggr(a_mv[:, j, :], a_st[:, j, :])
                ins.then_inc(s_avar, 1)

            def norm_shift(n, h, r):
                dve.wait_ge(s_ars, n + 1)
                if r >= 1:
                    dve.wait_ge(s_axn, n)
                nc.vector.scalar_tensor_tensor(out=a_rs[:, :, 0:1], in0=a_mv[:, :, 0:1], scalar=-1.0,
                                               in1=a_rs[:, :, 1:2], op0=ALU.mult, op1=ALU.mult).then_inc(s_ash, 1)

            def attend(n, h, r):
                early, late = r < NBAT, r >= 1
                b, rb = n - 1, r - 1
                hb = h - 1 if r % 2 == 0 else h
                hn = h if r % 2 == 0 else h + 1
                if late:
                    dve.wait_ge(s_kvps, b + 1)
                    if rb >= 1:
                        dve.wait_ge(s_ops, b)
                    nc.vector.tensor_tensor(kv[:, :, :], ps[:, 3, 0:D].rearrange("p (m e) -> p m e", e=P),
                                            same_head[:, None, :].to_broadcast([P, KD, P]),
                                            ALU.mult).then_inc(s_kv, 1)
                if early:
                    dve.wait_ge(s_axhi, n + 1)
                    nc.vector.tensor_tensor(a_xT_lo[:, :, :], feat_banks(0), a_xT_hi[:, :, :],
                                            ALU.subtract).then_inc(s_axlo, 1)
                if late:
                    dve.wait_ge(s_ops, b + 1)
                    dve.wait_ge(s_z, b + 1)
                    if rb >= 1:
                        dve.wait_ge(s_otp, b)
                    nc.vector.tensor_tensor(o_tok.rearrange("p (g e) -> p g e", e=HEAD_DIM),
                                            tok_banks(2).rearrange("p j (g e) -> p (j g) e", e=HEAD_DIM),
                                            zr[rb % 2][:, :, None].to_broadcast([P, NJ * heads, HEAD_DIM]),
                                            ALU.mult).then_inc(s_o, 1)
                if early:
                    for c in range(2 * KD):
                        dve.wait_ge(s_qkps, 2 * KD * n + c + 1)
                        if c == 0 and r >= 1:
                            dve.wait_ge(s_fps, 2 * KD * n)
                        nc.vector.tensor_scalar(qk[:, c, :], ps[:, 4 + c, :], QSCALE / W_SCALE, qk_bias[:, c:c + 1],
                                                ALU.mult, ALU.add).then_inc(s_qk, 1)
                if r < NBAT - 1:
                    norm_stats(n + 1, hn, r + 1)
                if late:
                    dve.wait_ge(s_ohi, b + 1)
                    nc.vector.tensor_tensor(oT_lo, feat_banks(0), oT_hi, ALU.subtract).then_inc(s_olo, 1)
                if early:
                    dve.wait_ge(s_vps, n + 1)
                    if r >= 2:
                        dve.wait_ge(s_kvps, n - 1)
                    nc.vector.scalar_tensor_tensor(out=vt[r % 2][:, :, :], in0=tok_banks(2), scalar=1.0 / W_SCALE,
                                                   in1=bv_sb[:, :, :].to_broadcast([P, NJ, D]),
                                                   op0=ALU.mult, op1=ALU.add).then_inc(s_v, 1)
                if r < NBAT - 1:
                    norm_shift(n + 1, hn, r + 1)
                if late:
                    dve.wait_ge(s_yps, b + 1)
                    dve.wait_ge(s_xb, b + 1)
                    if rb >= 2:
                        dve.wait_ge(s_rscat[rb % 2], 16 * NJ * hb)
                        dve.wait_ge(s_keep[rb % 2], 16 * hb)
                    nc.vector.scalar_tensor_tensor(out=rows[rb % 2][:, :, 0:D], in0=tok_banks(0), scalar=1.0 / W_SCALE,
                                                   in1=xb[rb % 2][:, :, :], op0=ALU.mult,
                                                   op1=ALU.add).then_inc(s_x2, 1)
                    route_stats(NBAT + b, NBAT // 2 + hb, NBAT + rb)
                    route_shift(NBAT + b, NBAT // 2 + hb, NBAT + rb)
                    route_low(NBAT + b, NBAT // 2 + hb, NBAT + rb)
                if early:
                    dve.wait_ge(s_zps, n + 1)
                    nc.vector.tensor_scalar(zt[:, :], ps[:, 0, 0:NJ * heads], EPS_Z, None, ALU.add).then_inc(s_zt, 1)
                    dve.wait_ge(s_zt, n + 1)
                    nc.vector.reciprocal(zr[r % 2][:, :], zt[:, :]).then_inc(s_z, 1)
                if late:
                    route_choose(NBAT + b, NBAT // 2 + hb, NBAT + rb)
                    route_seen(NBAT + b, NBAT // 2 + hb, NBAT + rb)
                    route_place(NBAT + b, NBAT // 2 + hb, NBAT + rb)

            dve.wait_ge(s_const, N_CONST + 4)
            dve.wait_ge(s_wT, 6)
            dve.wait_ge(s_rcnt, NBAT)
            nc.vector.memset(r_seen[0][:, 0, :], 0.0).then_inc(s_zero, 1)
            norm_stats(0, 0, 0)
            norm_shift(0, 0, 0)
            steps(dve, 0, 3, NBAT - 1, NBAT + 1, attend)
            w1_low(E, E // 2, E)
            slots_norm(E, E // 2, E)
            slots_T_low(E, E // 2, E)
            steps(dve, E, E, 2 * E - 2, 2 * E, expert)


_INS = ["L0_attn_x", "L0_attn_Wq", "L0_attn_bq", "L0_attn_Wk", "L0_attn_bk", "L0_attn_Wv", "L0_attn_bv",
        "L0_attn_Wo", "L0_attn_bo", "L0_attn_R", "L0_ffn_wg", "L0_ffn_w1", "L0_ffn_b1", "L0_ffn_w2", "L0_ffn_b2"]
_OUTS = [((8, 512, 256), "float32")]


def kernel(**inputs):
    import numpy as _np
    import concourse.bacc as _bacc
    from concourse import mybir as _mybir
    from concourse.bass_utils import run_bass_kernel_spmd as _run

    nc = _bacc.Bacc("TRN2", target_bir_lowering=False, num_devices=1)
    arrays, args = {}, []
    for name in _INS:
        a = _np.ascontiguousarray(inputs[name])
        arrays[f"in_{name}_dram"] = a
        args.append(nc.dram_tensor(f"in_{name}_dram", a.shape, _mybir.dt.from_np(a.dtype), kind="ExternalInput").ap())
    for i, (shape, dtype) in enumerate(_OUTS):
        dt = _mybir.dt.from_np(_np.dtype(dtype))
        args.append(nc.dram_tensor(f"out_{i}_dram", shape, dt, kind="ExternalOutput").ap())
    macaron_kernel(nc, *args)
    r = _run(nc, [arrays], core_ids=[0])
    got = tuple(r.results[0][f"out_{i}_dram"] for i in range(len(_OUTS)))
    return got[0]
```

```python
from contextlib import ExitStack

import concourse.bass as bass
from concourse import mybir

F32 = mybir.dt.float32
BF16 = mybir.dt.bfloat16
F16 = mybir.dt.float16
I32 = mybir.dt.int32
ALU = mybir.AluOpType
ACT = mybir.ActivationFunctionType
AX = mybir.AxisListType

P = 128
HEAD_DIM = 16
EPS_LN = 1e-5
EPS_Z = 1e-8
CAPACITY_FACTOR = 1.25
FAR = 1.0e6
C_GATE, C_ID, C_SHIFT, C_RSTD, EXTRA = 0, 1, 2, 3, 4
W_SCALE, H_SCALE = 64.0, 8.0


def macaron_kernel(nc, x, Wq, bq, Wk, bk, Wv, bv, Wo, bo, R, wg, w1, b1, w2, b2, out):
    NBAT, SEQ, D = x.shape
    E, _, F = w1.shape
    T = NBAT * SEQ
    KD = D // P
    NJ = SEQ // P
    FM = F // P
    CAP = int(CAPACITY_FACTOR * T / E)
    NS = CAP // P
    HALF = CAP // 2
    SLOTS = E * CAP
    ROW = D + EXTRA
    QSCALE = 1.0 / float(HEAD_DIM) ** 0.5
    GT, ID, SHIFT, RSTD = D + C_GATE, D + C_ID, D + C_SHIFT, D + C_RSTD

    x_rows = x.rearrange("b s d -> (b s) d")
    out_rows = out.rearrange("b s d -> (b s) d")
    x1_rows = nc.dram_tensor("x1_rows", [T, D], F32).ap()
    routed = [nc.dram_tensor(f"routed{i}", [SLOTS, ROW], F32).ap() for i in range(2)]
    after_ffn = [x1_rows, out_rows]

    with ExitStack() as ctx:
        def sb(name, shape, dt=F32):
            return ctx.enter_context(nc.sbuf_tensor(name, shape, dt))

        def sem(name):
            return ctx.enter_context(nc.semaphore(name))

        def sem2(name):
            return [sem(f"{name}_even"), sem(f"{name}_odd")]

        ident = sb("ident", [P, P])
        ones = sb("ones", [P, P])
        ones_b = sb("ones_b", [P, P], BF16)
        upto = sb("upto", [P, P], BF16)
        same_head = sb("same_head", [P, P])
        minus_half_head = sb("minus_half_head", [P, P])
        rank_i = sb("rank_i", [P, E], I32)
        rank = sb("rank", [P, E])
        ids_i = sb("ids_i", [P, T // P], I32)
        ids = sb("ids", [P, T // P])
        exponent = sb("exponent", [P, NJ])
        eps = sb("eps", [P, NJ])
        filler = sb("filler", [P, 1, ROW])
        w_raw = sb("w_raw", [P, 4, KD, D])
        wT_hi = sb("wT_hi", [P, 4, KD, D], F16)
        wT_lo = sb("wT_lo", [P, 4, KD, D], F16)
        wg_sb = sb("wg_sb", [P, KD, E])
        wg_hi = sb("wg_hi", [P, KD, E], F16)
        wg_lo = sb("wg_lo", [P, KD, E], F16)
        r_heads = sb("r_heads", [P, P])
        bias_rows = sb("bias_rows", [E * FM + 2 * KD, P])
        b1_cols = sb("b1_cols", [P, E * FM])
        qk_bias = sb("qk_bias", [P, 2 * KD])
        bv_sb = sb("bv_sb", [P, 1, D])
        bo_sb = sb("bo_sb", [P, 1, D])
        b2_sb = sb("b2_sb", [P, E, D])
        rows_first = sb("rows_first", [P, NBAT, NJ, ROW])
        rows = [sb(f"rows{i}", [P, NJ, ROW]) for i in range(2)]
        r_st = [sb(f"r_st{i}", [P, NJ, 6]) for i in range(2)]
        mv_first = sb("mv_first", [P, NBAT, NJ, 2])
        r_mv = [sb(f"r_mv{i}", [P, NJ, 2]) for i in range(2)]
        r_xn_both = sb("r_xn_both", [P, 2 * NJ * D])
        r_xn = [r_xn_both[:, i * NJ * D:(i + 1) * NJ * D].rearrange("p (j d) -> p j d", j=NJ) for i in range(2)]
        r_xT_hi = sb("r_xT_hi", [P, KD, SEQ], F16)
        r_xT_lo = sb("r_xT_lo", [P, KD, SEQ], F16)
        r_top = sb("r_top", [P, NJ])
        r_eq = sb("r_eq", [P, NJ, E])
        r_dl = sb("r_dl", [P, NJ, E])
        r_sc = sb("r_sc", [P, NJ, E])
        r_best = [sb(f"r_best{i}", [P, NJ]) for i in range(2)]
        r_oh = [sb(f"r_oh{i}", [P, NJ, E], BF16) for i in range(2)]
        r_sumj = sb("r_sumj", [P, E], BF16)
        r_seen = [sb(f"r_seen{i}", [P, 1, E], BF16) for i in range(2)]
        r_ex = sb("r_ex", [P, NJ, E])
        r_sum = sb("r_sum", [P, NJ])
        r_inv = sb("r_inv", [P, NJ])
        r_pm = sb("r_pm", [P, NJ, E])
        r_pos = sb("r_pos", [P, NJ])
        r_slot = sb("r_slot", [P, NJ])
        r_over = sb("r_over", [P, NJ])
        idx_first = sb("idx_first", [P, NBAT, NJ], I32)
        r_idx = [sb(f"r_idx{i}", [P, NJ], I32) for i in range(2)]
        w1_sb = [sb(f"w1_sb{i}", [P, KD, F]) for i in range(2)]
        w2_sb = [sb(f"w2_sb{i}", [P, FM, D]) for i in range(2)]
        xe = [sb(f"xe{i}", [P, NS, ROW]) for i in range(2)]
        xs = sb("xs", [P, NS, D])
        arena = sb("arena", [P, FM * CAP])

        def half_precision(words):
            halves = words.bitcast(F16)
            n = halves.shape[-1] // 2
            return [halves[:, i * n:(i + 1) * n] for i in range(2)]

        hT_hi, hT_lo = [v.rearrange("p (m t) -> p m t", m=FM) for v in half_precision(arena[:, :])]
        h_full = r_xn_both[:, 0:2 * CAP].rearrange("p (i t) -> p i t", i=2)
        xT_hi = sb("xT_hi", [P, KD, CAP], F16)
        xT_lo = sb("xT_lo", [P, KD, CAP], F16)
        w1_hi = sb("w1_hi", [P, KD, F], F16)
        w1_lo = sb("w1_lo", [P, KD, F], F16)
        w2_hi = sb("w2_hi", [P, FM, D], F16)
        w2_lo = sb("w2_lo", [P, FM, D], F16)
        y_b = sb("y_b", [P, 2, D])
        y_rows = [sb(f"y_rows{i}", [P, NS, D]) for i in range(2)]
        y_idx = [sb(f"y_idx{i}", [P, NS], I32) for i in range(2)]
        x1 = [sb(f"x1_{i}", [P, NJ, D]) for i in range(2)]
        a_st = sb("a_st", [P, NJ, 6])
        a_mv = sb("a_mv", [P, NJ, 2])
        a_rs = sb("a_rs", [P, NJ, 2])
        a_xn = sb("a_xn", [P, NJ, D])
        a_xT_hi = sb("a_xT_hi", [P, KD, SEQ], F16)
        a_xT_lo = sb("a_xT_lo", [P, KD, SEQ], F16)
        assert FM * CAP >= (2 * KD + 3 * KD) * SEQ

        def in_arena(block, n):
            return arena[:, block * SEQ:(block + n) * SEQ].rearrange("p (k t) -> p k t", k=n)

        qk = w_raw[:, :, :, :].rearrange("p w m d -> p (w m d)").rearrange("p (k t) -> p k t", k=2 * KD)
        qk2 = in_arena(0, 2 * KD)
        kf = in_arena(2 * KD, KD)
        o_tok = in_arena(3 * KD, KD).rearrange("p k t -> p (k t)")
        oT_hi, oT_lo = [v.rearrange("p (k t) -> p k t", k=KD)
                        for v in half_precision(arena[:, 4 * KD * SEQ:5 * KD * SEQ])]
        xn_first = [arena[:, (KD + i * KD) * SEQ:(2 * KD + i * KD) * SEQ].rearrange("p (j d) -> p j d", d=D)
                    for i in range(4)]
        xT_first = [v.rearrange("p (k t) -> p k t", k=KD) for v in half_precision(arena[:, 0:KD * SEQ])]

        spare_rows = rows_first[:, :, :, :].rearrange("p n j d -> p (n j d)")

        def in_rows(block):
            return spare_rows[:, block * NJ * D:(block + 1) * NJ * D]

        qf = [in_rows(i).rearrange("p (k t) -> p k t", k=KD) for i in range(2)]
        kt = [in_rows(2 + i).rearrange("p (j d) -> p j d", j=NJ) for i in range(2)]
        vt = [in_rows(4 + i).rearrange("p (j d) -> p j d", j=NJ) for i in range(2)]
        xb = [in_rows(6 + i).rearrange("p (j d) -> p j d", j=NJ) for i in range(2)]
        NH = P // HEAD_DIM
        zt = sb("zt", [P, NJ * KD, NH])
        zr = sb("zr", [P, NJ * KD, NH])
        kv = sb("kv", [P, KD, P + NH])

        ps = ctx.enter_context(nc.psum_tensor("ps", [P, 8, 512], F32))

        OUT_BANKS = [(2 + i, 3 * i, min(3, NJ * KD - 3 * i)) for i in range((NJ * KD + 2) // 3)]

        def tok_banks(b):
            return ps[:, b:b + 2, :].rearrange("p b (j d) -> p (b j) d", d=D)

        s_const = sem("s_const")
        s_zero = sem("s_zero")
        s_rzero = sem("s_rzero")
        s_wload = sem("s_wload")
        s_rload = sem("s_rload")
        s_bload = sem("s_bload")
        s_wg = sem("s_wg")
        s_fill = sem2("s_fill")
        s_base = sem("s_base")
        s_wT_pe = sem("s_wT_pe")
        s_wT = sem("s_wT")
        s_wTlo = sem("s_wTlo")
        s_wghi = sem("s_wghi")
        s_wglo = sem("s_wglo")
        s_rx = [sem(f"s_rx{n}") for n in range(NBAT)]
        s_x2 = sem("s_x2")
        s_rst = sem("s_rst")
        s_rvar = sem("s_rvar")
        s_rve = sem("s_rve")
        s_rsh = sem("s_rsh")
        s_rrs = sem("s_rrs")
        s_rid_first = sem("s_rid_first")
        s_rid = sem("s_rid")
        s_rxn = sem("s_rxn")
        s_rtp = sem("s_rtp")
        s_rxhi = sem("s_rxhi")
        s_rxlo = sem("s_rxlo")
        s_rlg = sem("s_rlg")
        s_rtop = sem("s_rtop")
        s_req = sem("s_req")
        s_rdl = sem("s_rdl")
        s_rsc = sem("s_rsc")
        s_rbest = sem("s_rbest")
        s_roh = sem("s_roh")
        s_rsumj = sem("s_rsumj")
        s_rseen = sem("s_rseen")
        s_rex = sem("s_rex")
        s_rsum = sem("s_rsum")
        s_rinv = sem("s_rinv")
        s_rgate = sem("s_rgate")
        s_rcnt = sem("s_rcnt")
        s_rpm = sem("s_rpm")
        s_rpos = sem("s_rpos")
        s_rslot = sem("s_rslot")
        s_rover = sem("s_rover")
        s_ridx = sem("s_ridx")
        s_rscat_first = sem("s_rscat_first")
        s_rscat = sem2("s_rscat")
        s_keep = sem2("s_keep")
        s_w1 = sem2("s_w1")
        s_w2 = sem2("s_w2")
        s_xe = sem2("s_xe")
        s_xe_first = [sem(f"s_xe_first{i}") for i in range(2)]
        s_xs = sem("s_xs")
        s_yid = sem("s_yid")
        s_xtp = sem("s_xtp")
        s_xhi = sem("s_xhi")
        s_xlo = sem("s_xlo")
        s_w1hi = sem("s_w1hi")
        s_w1lo = sem("s_w1lo")
        s_w2hi = sem("s_w2hi")
        s_w2lo = sem("s_w2lo")
        s_h = sem("s_h")
        s_hf = sem("s_hf")
        s_hhi = sem("s_hhi")
        s_hlo = sem("s_hlo")
        s_y = sem("s_y")
        s_yb = sem("s_yb")
        s_yrow = sem("s_yrow")
        s_yscat = sem2("s_yscat")
        s_ax = sem2("s_ax")
        s_ax_first = [sem(f"s_ax_first{i}") for i in range(2)]
        s_ast = sem("s_ast")
        s_avar = sem("s_avar")
        s_ave = sem("s_ave")
        s_ars = sem("s_ars")
        s_ash = sem("s_ash")
        s_axn = sem("s_axn")
        s_xb = sem("s_xb")
        s_atp = sem("s_atp")
        s_axhi = sem("s_axhi")
        s_axlo = sem("s_axlo")
        s_qkps = sem("s_qkps")
        s_qk = sem("s_qk")
        s_qk2 = sem("s_qk2")
        s_vps = sem("s_vps")
        s_v = sem("s_v")
        s_fps = sem("s_fps")
        s_f = sem("s_f")
        s_zt = sem("s_zt")
        s_z = sem("s_z")
        s_ktps = sem("s_ktps")
        s_kt = sem("s_kt")
        s_kvps = sem("s_kvps")
        s_kv = sem("s_kv")
        s_ops = sem("s_ops")
        s_o = sem("s_o")
        s_otp = sem("s_otp")
        s_ohi = sem("s_ohi")
        s_olo = sem("s_olo")
        s_yps = sem("s_yps")

        s_aggr_go = sem("s_aggr_go")
        s_scatter_go = sem("s_scatter_go")
        s_split_go = sem("s_split_go")

        LOGITS, COUNTS = [3, 6], [2, 7]
        SLOT_PIECES = [(0, 2), (2, NS)]
        ROW_PIECES = [(0, NJ // 2), (NJ // 2, NJ)]
        WARM_ROUTED, WARM_SLOTS, WARM_X1, WARM_TAIL = [60, 36], 6, [40, 9], [7, 8, 18]
        H_BANKS = [0, 2, 6]
        T_BANKS = [6, 7, 0]
        N_CONST = 13
        ALL_ROUTED = 16 * NJ * NBAT // 2
        ALL_SLOTS = 16 * NS * E // 2

        def steps(eng, first, loop_from, loop_to, last, body):
            for n in range(first, loop_from):
                body(n, n // 2, n)
            with eng.Fori(0, (loop_to - loop_from) // 2) as i:
                for u in range(2):
                    body(loop_from + u + 2 * i, (loop_from + u) // 2 + i, loop_from + u)
            for n in range(loop_to, last):
                body(n, n // 2, n)

        def route_rows(r):
            return rows_first[:, r, :, :] if r < NBAT else rows[r % 2]

        def route_xn(r):
            return xn_first[r % 4] if r < NBAT else r_xn[r % 2]

        def route_mv(r):
            return mv_first[:, r, :, :] if r < NBAT else r_mv[r % 2]

        def route_xT(r):
            return xT_first if r < NBAT and r % 2 == 0 else [r_xT_hi[:, :, :], r_xT_lo[:, :, :]]

        def route_bank(r):
            return 0 if r < NBAT and r % 2 == 0 else 4

        def route_idx(r):
            return idx_first[:, r, :] if r < NBAT else r_idx[r % 2]

        QK_ORDER = [1, 2, 0, 3]

        block = ctx.enter_context(nc.Block())

        @block.sync
        def _(sp):
            def load_rows(n):
                sp.dma_start(rows_first[:, n, :, 0:D],
                             x_rows[n * SEQ:(n + 1) * SEQ, :].rearrange("(j p) d -> p j d", p=P)
                             ).then_inc(s_rx[n], 16)

            def fill(ph):
                sp.dma_start(routed[ph].rearrange("(n p) d -> p n d", p=P),
                             filler[:, :, :].to_broadcast([P, SLOTS // P, ROW])).then_inc(s_fill[ph], 16)

            def load_weights(n, h, r):
                e = n - (r // E) * E
                if r >= 2:
                    sp.wait_ge(s_w1lo, KD * (n - 1))
                sp.dma_start(w1_sb[r % 2][:, :, :],
                             w1[bass.ds(e, 1), :, :].rearrange("e (k p) f -> p (e k) f", p=P)
                             ).then_inc(s_w1[r % 2], 16)
                if r >= 2:
                    sp.wait_ge(s_w2lo, 2 * (n - 1))
                sp.dma_start(w2_sb[r % 2][:, :, :],
                             w2[bass.ds(e, 1), :, :].rearrange("e (m p) d -> p (e m) d", p=P)
                             ).then_inc(s_w2[r % 2], 16)

            def load_slots(n, h, r):
                ph = r // E
                if r >= 2:
                    sp.wait_ge(s_yrow, NS * (n - 1))
                    sp.wait_ge(s_yid, n - 1)
                sp.dma_start(xe[r % 2][:, :, :],
                             routed[ph][bass.ds((n - ph * E) * CAP, CAP), :].rearrange("(s p) d -> p s d", p=P)
                             ).then_inc(s_xe[r % 2], 16)

            def load_first_slots(ph):
                for i, (lo, hi) in enumerate(SLOT_PIECES):
                    sp.dma_start(xe[0][:, lo:hi, :],
                                 routed[ph][lo * P:hi * P, :].rearrange("(s p) d -> p s d", p=P)
                                 ).then_inc(s_xe_first[i], 16)

            def load_both(n, h, r):
                load_weights(n, h, r)
                load_slots(n, h, r)

            load_rows(0)
            load_rows(1)
            for i, w in enumerate((Wq, Wk, Wv, Wo)):
                sp.dma_start(w_raw[:, i, :, :], w.rearrange("(m p) d -> p m d", p=P)).then_inc(s_wload, 16)
            sp.dma_start(bias_rows[0:E * FM, :], b1.rearrange("e (m p) -> (e m) p", p=P)).then_inc(s_wload, 16)
            for i, b in enumerate((bq, bk)):
                lo = E * FM + i * KD
                sp.dma_start(bias_rows[lo:lo + KD, :], b.rearrange("(m p) -> m p", p=P)).then_inc(s_wload, 16)
            sp.dma_start(wg_sb[:, :, :], wg.rearrange("(k p) e -> p k e", p=P)).then_inc(s_wg, 16)
            for n in range(2, NBAT):
                load_rows(n)
            sp.wait_ge(s_const, N_CONST)
            fill(0)
            load_weights(0, 0, 0)
            load_weights(1, 0, 1)
            sp.dma_start(bv_sb[:, 0, :], bv.rearrange("(a d) -> a d", a=1).to_broadcast([P, D])).then_inc(s_bload, 16)
            sp.dma_start(bo_sb[:, 0, :], bo.rearrange("(a d) -> a d", a=1).to_broadcast([P, D])).then_inc(s_bload, 16)
            sp.dma_start(b2_sb[:, :, :].rearrange("p e d -> p (e d)"),
                         b2.rearrange("(a e) d -> a (e d)", a=1).to_broadcast([P, E * D])).then_inc(s_bload, 16)
            sp.wait_ge(s_rzero, 1)
            for hd in range(P // HEAD_DIM):
                at = slice(hd * HEAD_DIM, (hd + 1) * HEAD_DIM)
                sp.dma_start(r_heads[at, at], R).then_inc(s_rload, 16)
            sp.wait_ge(s_rscat_first, 16 * NJ * NBAT)
            load_first_slots(0)
            load_slots(1, 0, 1)
            sp.dma_start(x1_rows, x_rows).then_inc(s_base, 16)
            fill(1)
            steps(sp, 2, 2, E, E, load_both)

            def load_x1(n, h, r):
                if r >= 2:
                    sp.wait_ge(s_axn, NJ * (n - 1))
                    sp.wait_ge(s_xb, n - 1)
                sp.dma_start(x1[r % 2][:, :, :],
                             x1_rows[bass.ds(n * SEQ, SEQ), :].rearrange("(j p) d -> p j d", p=P)
                             ).then_inc(s_ax[r % 2], 16)

            def store_x2(n, h, r):
                sp.wait_ge(s_x2, 2 * (n + 1))
                sp.dma_start(out_rows[bass.ds(n * SEQ, SEQ), :].rearrange("(j p) d -> p j d", p=P),
                             rows[r % 2][:, :, 0:D]).then_inc(s_keep[r % 2], 16)

            for q in s_yscat:
                sp.wait_ge(q, ALL_SLOTS)
            for i, (lo, hi) in enumerate(ROW_PIECES):
                sp.dma_start(x1[0][:, lo:hi, :],
                             x1_rows[lo * P:hi * P, :].rearrange("(j p) d -> p j d", p=P)
                             ).then_inc(s_ax_first[i], 16)
            load_x1(1, 0, 1)
            load_weights(E, E // 2, E)
            load_weights(E + 1, E // 2, E + 1)

            def attention_traffic(n, h, r):
                load_x1(n, h, r)
                store_x2(n - 2, h - 1, r - 2)

            steps(sp, 2, 2, NBAT, NBAT, attention_traffic)
            store_x2(NBAT - 2, NBAT // 2 - 1, NBAT - 2)
            store_x2(NBAT - 1, NBAT // 2 - 1, NBAT - 1)
            for q in s_rscat:
                sp.wait_ge(q, ALL_ROUTED)
            sp.wait_ge(s_yrow, NS * (E - 1))
            sp.wait_ge(s_yid, E - 1)
            load_first_slots(1)
            load_slots(E + 1, E // 2, E + 1)
            steps(sp, E + 2, E + 2, 2 * E, 2 * E, load_both)
            for q in s_keep:
                sp.wait_ge(q, 16 * NBAT // 2)
            for q in s_yscat:
                sp.wait_ge(q, 2 * ALL_SLOTS)

        @block.gpsimd
        def _(pool):
            pool.memset(filler[:, :, :], 0.0).then_inc(s_const, 1)
            pool.memset(ident[:, :], 0.0).then_inc(s_const, 1)
            pool.memset(ones[:, :], 1.0).then_inc(s_const, 1)
            pool.memset(ones_b[:, :], 1.0).then_inc(s_const, 1)
            pool.memset(exponent[:, :], -0.5).then_inc(s_const, 1)
            pool.memset(eps[:, :], EPS_LN).then_inc(s_const, 1)
            pool.iota(rank_i[:, :], pattern=[[-1, E]], base=E, channel_multiplier=0).then_inc(s_const, 1)
            pool.iota(ids_i[:, :], pattern=[[P, T // P]], base=0, channel_multiplier=1).then_inc(s_const, 1)
            pool.wait_ge(s_const, 8)
            pool.memset(filler[:, :, ID:ID + 1], FAR).then_inc(s_const, 1)
            pool.affine_select(out=ident[:, :], in_=ident[:, :], compare_op=ALU.not_equal, fill=1.0,
                               base=0, pattern=[[-1, P]], channel_multiplier=1).then_inc(s_const, 1)
            pool.affine_select(out=upto[:, :], in_=ones_b[:, :], compare_op=ALU.is_ge, fill=0.0,
                               base=0, pattern=[[1, P]], channel_multiplier=-1).then_inc(s_const, 1)
            nh = NH
            pool.affine_select(out=minus_half_head[:, :], in_=ones[:, :], compare_op=ALU.is_ge, fill=0.0,
                               base=0, pattern=[[-HEAD_DIM, nh], [0, HEAD_DIM]],
                               channel_multiplier=1).then_inc(s_const, 1)
            pool.tensor_copy(ids[:, :], ids_i[:, :]).then_inc(s_const, 1)
            assert N_CONST == 13
            pool.wait_ge(s_const, N_CONST)
            pool.tensor_copy(rank[:, :], rank_i[:, :]).then_inc(s_const, 1)
            pool.affine_select(out=same_head[:, :], in_=minus_half_head[:, :], compare_op=ALU.is_ge, fill=0.0,
                               base=HEAD_DIM - 1, pattern=[[HEAD_DIM, nh], [0, HEAD_DIM]],
                               channel_multiplier=-1).then_inc(s_const, 1)
            pool.wait_ge(s_const, N_CONST + 2)
            pool.tensor_copy(kv[:, :, P:P + NH],
                             same_head[:, :].rearrange("p (a h d) -> p a h d", a=1, d=HEAD_DIM)[:, :, :, 0]
                             .to_broadcast([P, KD, NH])).then_inc(s_const, 1)
            pool.tensor_scalar(minus_half_head[:, :], same_head[:, :], -0.5, None, ALU.mult).then_inc(s_const, 1)

            def route_rstd(n, h, r):
                at = route_mv(r)[:, :, 1:2]
                pool.wait_ge(s_rvar, n + 1)
                pool.tensor_tensor(at, at, eps[:, :, None], ALU.add).then_inc(s_rve, 1)
                pool.wait_ge(s_rve, n + 1)
                pool.tensor_tensor(route_rows(r)[:, :, RSTD:RSTD + 1], at, exponent[:, :, None],
                                   ALU.pow).then_inc(s_rrs, 1)

            def route_scatter(n, h, r):
                ph = r // NBAT
                pool.wait_ge(s_fill[ph], 16)
                pool.wait_ge(s_ridx, n + 1)
                pool.wait_ge(s_rgate, n + 1)
                if r >= NBAT:
                    pool.wait_ge(s_rid, n - NBAT + 1)
                else:
                    pool.wait_ge(s_rid_first, 1)
                pool.wait_ge(s_rsh, n + 1)
                pool.sem_inc(s_scatter_go, 1)
                for j in range(NJ):
                    landed = s_rscat_first if ph == 0 else s_rscat[r % 2]
                    pool.indirect_dma_start(routed[ph], bass.IndirectOffsetOnAxis(ap=route_idx(r)[:, j:j + 1], axis=0),
                                            route_rows(r)[:, j, :], None, bounds_check=SLOTS - 1,
                                            oob_is_err=False).then_inc(landed, 16)

            for n in range(NBAT):
                route_rstd(n, n // 2, n)
            for n in range(NBAT):
                route_scatter(n, n // 2, n)

            def w2_high(n, h, r):
                pool.wait_ge(s_w2[r % 2], 16 * (h + 1))
                if r >= 1:
                    pool.wait_ge(s_y, NS * n)
                pool.sem_inc(s_split_go, 1)
                for i in range(2):
                    nc.gpsimd.tensor_scalar(w2_hi[:, i * FM // 2:(i + 1) * FM // 2, :],
                                            w2_sb[r % 2][:, i * FM // 2:(i + 1) * FM // 2, :],
                                            W_SCALE, None, ALU.mult).then_inc(s_w2hi, 1)

            def slots_out(n, h, r):
                ph = r // E
                pool.wait_ge(s_yid, n + 1)
                for s in range(NS):
                    pool.wait_ge(s_yrow, NS * n + s + 1)
                    pool.sem_inc(s_scatter_go, 1)
                    pool.indirect_dma_start(after_ffn[ph],
                                            bass.IndirectOffsetOnAxis(ap=y_idx[r % 2][:, s:s + 1], axis=0),
                                            y_rows[r % 2][:, s, :], None, bounds_check=T - 1,
                                            oob_is_err=False).then_inc(s_yscat[r % 2], 16)
                if r % E != E - 1:
                    w2_high(n + 1, h if r % 2 == 0 else h + 1, r + 1)

            w2_high(0, 0, 0)
            pool.wait_ge(s_base, 16)
            steps(pool, 0, 0, E - 2, E, slots_out)

            def add_bo(n, h, r):
                if r == 0:
                    for q in s_ax_first:
                        pool.wait_ge(q, 16)
                else:
                    pool.wait_ge(s_ax[r % 2], 16 * (h + r % 2))
                if r >= 2:
                    pool.wait_ge(s_x2, 2 * (n - 1))
                pool.tensor_tensor(xb[r % 2][:, :, :], x1[r % 2][:, :, :],
                                   bo_sb[:, :, :].to_broadcast([P, NJ, D]), ALU.add).then_inc(s_xb, 1)

            def norm_rstd(n, h, r):
                at = a_mv[:, :, 1:2]
                pool.wait_ge(s_avar, n + 1)
                pool.tensor_tensor(at, at, eps[:, :, None], ALU.add).then_inc(s_ave, 1)
                pool.wait_ge(s_ave, n + 1)
                if r >= 1:
                    pool.wait_ge(s_axn, NJ * n)
                pool.tensor_tensor(a_rs[:, :, 1:2], at, exponent[:, :, None], ALU.pow).then_inc(s_ars, 1)

            def attend(n, h, r):
                hb = h - 1 if r % 2 == 0 else h
                if r >= 2:
                    route_scatter(NBAT + n - 2, NBAT // 2 + h - 1, NBAT + r - 2)
                if r < NBAT - 1:
                    norm_rstd(n + 1, h, r + 1)
                if r < NBAT:
                    add_bo(n, h, r)
                if 1 <= r <= NBAT:
                    route_rstd(NBAT + n - 1, NBAT // 2 + hb, NBAT + r - 1)

            pool.wait_ge(s_bload, 48)
            norm_rstd(0, 0, 0)
            steps(pool, 0, 3, NBAT - 1, NBAT + 2, attend)
            w2_high(E, E // 2, E)
            for q in s_keep:
                pool.wait_ge(q, 16 * NBAT // 2)
            steps(pool, E, E, 2 * E - 2, 2 * E, slots_out)

        @block.scalar
        def _(act):
            for i in range(4):
                act.wait_ge(s_wT_pe, i + 1)
                nc.scalar.activation(wT_hi[:, i, :, :].rearrange("p k d -> p (k d)"), ps[:, i, :], ACT.Copy,
                                     scale=W_SCALE).then_inc(s_wT, 1)
            act.wait_ge(s_wT_pe, 5)
            nc.scalar.mul(b1_cols[:, :], ps[:, 4, 0:E * FM], H_SCALE).then_inc(s_wT, 1)
            nc.scalar.mul(qk_bias[:, :], ps[:, 4, E * FM:E * FM + 2 * KD], QSCALE).then_inc(s_wT, 1)

            def route_norm(n, h, r):
                at = route_rows(r)
                act.wait_ge(s_rsh, n + 1)
                if r >= NBAT + 2:
                    act.wait_ge(s_rtp, n - 1)
                elif 4 <= r < NBAT:
                    act.wait_ge(s_rtp, n - 3)
                for j in range(NJ):
                    nc.scalar.activation(route_xn(r)[:, j, :], at[:, j, 0:D], ACT.Identity,
                                               scale=at[:, j, RSTD:RSTD + 1], bias=at[:, j, SHIFT:SHIFT + 1]
                                               ).then_inc(s_rxn, 1)

            def route_evacuate(n, h, r):
                act.wait_ge(s_rtp, n + 1)
                if r >= NBAT:
                    act.wait_ge(s_rlg, n)
                elif r >= 2:
                    act.wait_ge(s_rlg, n - 1)
                for k in range(KD):
                    nc.scalar.copy(route_xT(r)[0][:, k, :], ps[:, route_bank(r) + k, :]).then_inc(s_rxhi, 1)

            def route_exp(n, h, r):
                act.wait_ge(s_rdl, n + 1)
                if r >= 1:
                    act.wait_ge(s_rsum, n)
                nc.scalar.activation(r_ex[:, :, :], r_dl[:, :, :], ACT.Exp,
                                     scale=1.0 / W_SCALE).then_inc(s_rex, 1)

            for n in range(4):
                route_norm(n, n // 2, n)
                if n == 1:
                    route_evacuate(0, 0, 0)
            for n in range(NBAT):
                if n + 1 < NBAT:
                    route_evacuate(n + 1, (n + 1) // 2, n + 1)
                if n + 4 < NBAT:
                    route_norm(n + 4, (n + 4) // 2, n + 4)
                route_exp(n, n // 2, n)

            def slots_T(n, h, r):
                for c in range((NS + 1) // 2):
                    w = min(2, NS - 2 * c) * P
                    act.wait_ge(s_xtp, 3 * n + c + 1)
                    nc.scalar.copy(xT_hi[:, :, 2 * c * P:2 * c * P + w],
                                   ps[:, T_BANKS[c], :].rearrange("p (k t) -> p k t", k=KD)[:, :, 0:w]
                                   ).then_inc(s_xhi, 1)

            def w1_high(n, h, r):
                act.wait_ge(s_w1[r % 2], 16 * (h + 1))
                if r >= 1:
                    act.wait_ge(s_h, FM * n)
                for k in range(KD):
                    nc.scalar.activation(w1_hi[:, k, :], w1_sb[r % 2][:, k, :], ACT.Copy,
                                         scale=W_SCALE).then_inc(s_w1hi, 1)

            def relu(n, h, r):
                if r >= 1:
                    act.wait_ge(s_y, NS * n)
                for m in range(FM):
                    act.wait_ge(s_h, FM * n + m + 1)
                    if r >= 1 or m >= 2:
                        act.wait_ge(s_hlo, FM * n + m - 1)
                    b = H_BANKS[m % 3]
                    for dst, done in ((hT_hi[:, m, :], s_hhi), (h_full[:, m % 2, :], s_hf)):
                        nc.scalar.activation(dst.rearrange("p (a t) -> p a t", a=2), ps[:, b:b + 2, 0:HALF],
                                             ACT.Relu, scale=H_SCALE / W_SCALE,
                                             bias=b1_cols[:, bass.ds((n - (r // E) * E) * FM + m, 1)]
                                             ).then_inc(done, 1)

            def expert(n, h, r):
                relu(n, h, r)
                if r % E != E - 1:
                    slots_T(n + 1, h, r + 1)
                    w1_high(n + 1, h if r % 2 == 0 else h + 1, r + 1)

            w1_high(0, 0, 0)
            slots_T(0, 0, 0)
            steps(act, 0, 2, E - 2, E, expert)

            def norm(n, h, r):
                act.wait_ge(s_ash, n + 1)
                if r >= 1:
                    act.wait_ge(s_atp, n)
                for j in range(NJ):
                    nc.scalar.activation(a_xn[:, j, :], x1[r % 2][:, j, :], ACT.Identity,
                                         scale=a_rs[:, j, 1:2], bias=a_rs[:, j, 0:1]).then_inc(s_axn, 1)

            def attend(n, h, r):
                early, late, placed = r < NBAT, 1 <= r <= NBAT, r >= 2
                if early:
                    act.wait_ge(s_atp, n + 1)
                    if r >= 1:
                        act.wait_ge(s_vps, n)
                    for k in range(KD):
                        nc.scalar.copy(a_xT_hi[:, k, :], ps[:, k, :]).then_inc(s_axhi, 1)
                if placed:
                    route_exp(NBAT + n - 2, h, NBAT + r - 2)
                if late:
                    act.wait_ge(s_otp, n)
                    if r >= 2:
                        act.wait_ge(s_yps, 2 * (n - 1))
                    for k in range(KD):
                        nc.scalar.copy(oT_hi[:, k, :], ps[:, k, :]).then_inc(s_ohi, 1)
                if early:
                    for i, c in enumerate(QK_ORDER):
                        act.wait_ge(s_qk, 2 * KD * n + i + 1)
                        if i == 0 and r >= 1:
                            act.wait_ge(s_fps, 2 * KD * n)
                        nc.scalar.activation(qk2[:, c, :], qk[:, c, :], ACT.Square).then_inc(s_qk2, 1)
                if r < NBAT - 1:
                    norm(n + 1, h, r + 1)
                if early:
                    for c in range(KD):
                        act.wait_ge(s_fps, 2 * KD * n + c + 1)
                        if c == 0 and r >= 2:
                            act.wait_ge(s_ops, n - 1)
                        nc.scalar.activation(qf[r % 2][:, c, :], ps[:, 4 + c, :], ACT.Exp).then_inc(s_f, 1)
                if late:
                    route_norm(NBAT + n - 1, h, NBAT + r - 1)
                if early:
                    for c in range(KD):
                        act.wait_ge(s_fps, 2 * KD * n + KD + c + 1)
                        if c == 0 and r >= 1:
                            act.wait_ge(s_ktps, n)
                        nc.scalar.activation(kf[:, c, :], ps[:, 4 + KD + c, :], ACT.Exp).then_inc(s_f, 1)
                if late:
                    route_evacuate(NBAT + n - 1, h, NBAT + r - 1)
                if early:
                    act.wait_ge(s_ktps, n + 1)
                    if r >= 2:
                        act.wait_ge(s_kvps, n - 1)
                    nc.scalar.copy(kt[r % 2][:, :, :], tok_banks(6)).then_inc(s_kt, 1)

            norm(0, 0, 0)
            steps(act, 0, 3, NBAT - 1, NBAT + 2, attend)
            w1_high(E, E // 2, E)
            slots_T(E, E // 2, E)
            steps(act, E, E, 2 * E - 2, 2 * E, expert)

        @block.tensor
        def _(pe):
            pe.wait_ge(s_const, N_CONST)
            pe.wait_ge(s_wload, 16 * 7)
            for i in range(4):
                for k in range(KD):
                    for m in range(KD):
                        mm = nc.tensor.transpose(ps[:, i, k * D + m * P:k * D + (m + 1) * P],
                                                 w_raw[:, i, m, k * P:(k + 1) * P], ident[:, :])
                mm.then_inc(s_wT_pe, 1)
            nb = E * FM + 2 * KD
            nc.tensor.transpose(ps[:, 4, 0:nb], bias_rows[:, :], ident[0:nb, 0:nb]).then_inc(s_wT_pe, 1)
            pe.wait_ge(s_wT, 6)
            pe.wait_ge(s_wTlo, 4)
            pe.wait_ge(s_wglo, 1)

            def product(dst, pairs):
                for i, (stationary, moving) in enumerate(pairs):
                    mm = nc.tensor.matmul(dst, stationary, moving, start=(i == 0), stop=(i == len(pairs) - 1))
                return mm

            def keep_warm(bank, products):
                for _ in range(products):
                    nc.tensor.matmul(ps[:, bank, :], wT_hi[:, 0, 0, 0:P],
                                     wT_hi[:, 0, :, :].rearrange("p k d -> p (k d)"), start=True, stop=True)

            def rows_T(n, h, r):
                b = route_bank(r)
                if r > NBAT:
                    pe.wait_ge(s_rxlo, KD * n)
                elif 2 <= r < NBAT:
                    pe.wait_ge(s_rxlo, KD * (n - 1))
                for j in range(NJ):
                    pe.wait_ge(s_rxn, NJ * n + j + 1)
                    for k in range(KD):
                        mm = nc.tensor.transpose(ps[:, b + k, j * P:(j + 1) * P],
                                                 route_xn(r)[:, j, k * P:(k + 1) * P], ident[:, :])
                mm.then_inc(s_rtp, 1)

            def logits(n, h, r):
                pe.wait_ge(s_rxlo, KD * (n + 1))
                if r >= 1:
                    pe.wait_ge(s_rdl, n)
                    pe.wait_ge(s_req, n)
                x_hi, x_lo = route_xT(r)
                for j in range(NJ):
                    mm = product(ps[:, LOGITS[r // NBAT], j * E:(j + 1) * E],
                                 [(x[:, k, j * P:(j + 1) * P], w[:, k, :]) for k in range(KD)
                                  for x, w in ((x_hi, wg_hi), (x_hi, wg_lo), (x_lo, wg_hi), (x_lo, wg_lo))])
                mm.then_inc(s_rlg, 1)

            def counts(n, h, r):
                pe.wait_ge(s_roh, n + 1)
                if r % NBAT == 0:
                    pe.wait_ge(s_zero, r // NBAT + 1)
                else:
                    pe.wait_ge(s_rseen, n - r // NBAT)
                if r >= 1:
                    pe.wait_ge(s_rpm, n)
                oh = r_oh[r % 2]
                dst = ps[:, COUNTS[r // NBAT], 0:NJ * E].rearrange("p (j e) -> p j e", e=E)
                nc.tensor.matmul(dst, upto[:, :], oh[:, :, :], start=True, stop=False)
                nc.tensor.matmul(dst, ones_b[:, :], r_seen[r % 2][:, :, :].to_broadcast([P, NJ, E]),
                                 start=False, stop=False)
                for back in range(1, NJ):
                    mm = nc.tensor.matmul(dst[:, back:NJ, :], ones_b[:, :], oh[:, 0:NJ - back, :],
                                          start=False, stop=(back == NJ - 1))
                mm.then_inc(s_rcnt, 1)

            rows_T(0, 0, 0)
            for n in range(NBAT + 1):
                if n + 1 < NBAT:
                    rows_T(n + 1, (n + 1) // 2, n + 1)
                if n < NBAT:
                    logits(n, n // 2, n)
                if n >= 1:
                    counts(n - 1, (n - 1) // 2, n - 1)

            def slots_T(n, h, r):
                if r % E:
                    pe.wait_ge(s_hf, FM * n - 2)
                for c in range((NS + 1) // 2):
                    if c == 2 and r % E:
                        pe.wait_ge(s_hf, FM * n - 1)
                    for s in range(2 * c, min(2 * c + 2, NS)):
                        pe.wait_ge(s_xs, NS * n + s + 1)
                        for k in range(KD):
                            at = k * 2 * P + (s - 2 * c) * P
                            mm = nc.tensor.transpose(ps[:, T_BANKS[c], at:at + P],
                                                     xs[:, s, k * P:(k + 1) * P], ident[:, :])
                    mm.then_inc(s_xtp, 1)

            def hidden(n, h, r):
                pe.wait_ge(s_xlo, 3 * n + 3)
                pe.wait_ge(s_w1lo, KD * (n + 1))
                for m in range(FM):
                    if m >= 3:
                        pe.wait_ge(s_hf, FM * n + m - 2)
                    elif m < 2 and r >= 1:
                        pe.wait_ge(s_hf, FM * n + m - 1)
                    b = H_BANKS[m % 3]
                    parts = [(w1_hi, xT_hi), (w1_hi, xT_lo), (w1_lo, xT_hi)]
                    for k in range(KD):
                        for i, (w_part, x_part) in enumerate(parts):
                            for a in range(2):
                                mm = nc.tensor.matmul(ps[:, b + a, 0:HALF], w_part[:, k, m * P:(m + 1) * P],
                                                      x_part[:, k, a * HALF:(a + 1) * HALF],
                                                      start=(k == 0 and i == 0), stop=(k == KD - 1 and i == 2))
                    mm.then_inc(s_h, 1)

            def expert_out(n, h, r):
                pe.wait_ge(s_hhi, FM * (n + 1))
                pe.wait_ge(s_w2lo, 2 * (n + 1))
                for s in range(NS):
                    if r >= 1 or s >= 2:
                        pe.wait_ge(s_yb, NS * n + s - 1)
                    b = 4 + s % 2 if r % 2 == 0 else 4 + (s + 1) % 2
                    for w_part in (w2_hi, w2_lo):
                        for m in range(FM):
                            nc.tensor.matmul(ps[:, b, 0:D], hT_hi[:, m, s * P:(s + 1) * P], w_part[:, m, :],
                                             start=(m == 0 and w_part is w2_hi), stop=False)
                    if s == 0:
                        pe.wait_ge(s_hlo, FM * (n + 1))
                    for m in range(FM):
                        mm = nc.tensor.matmul(ps[:, b, 0:D], hT_lo[:, m, s * P:(s + 1) * P], w2_hi[:, m, :],
                                              start=False, stop=(m == FM - 1))
                    mm.then_inc(s_y, 1)

            def expert(n, h, r):
                hidden(n, h, r)
                if r % E != E - 1:
                    slots_T(n + 1, h, r + 1)
                expert_out(n, h, r)

            pe.wait_ge(s_scatter_go, NBAT)
            keep_warm(5, WARM_ROUTED[0])
            slots_T(0, 0, 0)
            keep_warm(5, WARM_SLOTS)
            steps(pe, 0, 2, E - 2, E, expert)

            def attend(n, h, r):
                early, late, placed = r < NBAT, 1 <= r <= NBAT, r >= 2
                b, rb = n - 1, r - 1
                if early:
                    if r >= 2:
                        pe.wait_ge(s_x2, 2 * (n - 1))
                    for j in range(NJ):
                        pe.wait_ge(s_axn, NJ * n + j + 1)
                        for k in range(KD):
                            mm = nc.tensor.transpose(ps[:, k, j * P:(j + 1) * P],
                                                     a_xn[:, j, k * P:(k + 1) * P], ident[:, :])
                    mm.then_inc(s_atp, 1)
                if r == 0:
                    keep_warm(7, WARM_X1[1])
                if late:
                    pe.wait_ge(s_kt, b + 1)
                    pe.wait_ge(s_v, b + 1)
                    for m in range(KD):
                        mm = product(ps[:, 2, m * P:(m + 1) * P],
                                     [(kt[rb % 2][:, j, m * P:(m + 1) * P], vt[rb % 2][:, j, m * P:(m + 1) * P])
                                      for j in range(NJ)])
                    mm.then_inc(s_kvps, 1)
                if placed:
                    logits(NBAT + n - 2, h, NBAT + r - 2)
                if late:
                    pe.wait_ge(s_kv, b + 1)
                    for bank, first, blocks in OUT_BANKS:
                        for g in range(first, first + blocks):
                            j, m = g // KD, g % KD
                            at = (g - first) * (P + NH)
                            mm = nc.tensor.matmul(ps[:, bank, at:at + P + NH],
                                                  qf[rb % 2][:, m, j * P:(j + 1) * P], kv[:, m, :],
                                                  start=True, stop=True)
                    mm.then_inc(s_ops, 1)
                if placed:
                    counts(NBAT + n - 2, h, NBAT + r - 2)
                if early:
                    pe.wait_ge(s_axlo, KD * (n + 1))
                    if r >= 1:
                        pe.wait_ge(s_kt, n)
                    for i, c in enumerate(QK_ORDER):
                        w, m = c // KD, c % KD
                        if c == 0 and late:
                            pe.wait_ge(s_o, b + 1)
                        if c == 2 and placed:
                            pe.wait_ge(s_rdl, NBAT + n - 1)
                            pe.wait_ge(s_req, NBAT + n - 1)
                        if c == 3 and placed:
                            pe.wait_ge(s_rpm, NBAT + n - 1)
                        product(ps[:, 4 + c, :],
                                [(w_part[:, w, k, m * P:(m + 1) * P], x_part[:, k, :]) for k in range(KD)
                                 for w_part, x_part in ((wT_hi, a_xT_hi), (wT_hi, a_xT_lo), (wT_lo, a_xT_hi))]
                                ).then_inc(s_qkps, 1)
                if r == NBAT:
                    keep_warm(5, WARM_TAIL[0])
                if late:
                    pe.wait_ge(s_o, b + 1)
                    for j in range(NJ):
                        for k in range(KD):
                            mm = nc.tensor.transpose(ps[:, k, j * P:(j + 1) * P],
                                                     o_tok[:, j * D + k * P:j * D + (k + 1) * P], ident[:, :])
                    mm.then_inc(s_otp, 1)
                if early:
                    for j in range(NJ):
                        mm = product(tok_banks(2)[:, j, :],
                                     [(x_part[:, k, j * P:(j + 1) * P], w_part[:, 2, k, :]) for k in range(KD)
                                      for x_part, w_part in ((a_xT_hi, wT_hi), (a_xT_hi, wT_lo), (a_xT_lo, wT_hi))])
                    mm.then_inc(s_vps, 1)
                if r == NBAT:
                    keep_warm(5, WARM_TAIL[1])
                if late:
                    pe.wait_ge(s_olo, KD * (b + 1))
                    for j in range(NJ):
                        mm = product(tok_banks(0)[:, j, :],
                                     [(o_part[:, m, j * P:(j + 1) * P], w_part[:, 3, m, :]) for m in range(KD)
                                      for o_part, w_part in ((oT_hi, wT_hi), (oT_hi, wT_lo), (oT_lo, wT_hi))])
                        if j % 2 == 1:
                            mm.then_inc(s_yps, 1)
                if early:
                    for c in range(2 * KD):
                        if c == 0:
                            pe.wait_ge(s_qk, 2 * KD * (n + 1))
                        nc.tensor.matmul(ps[:, 4 + c, :], r_heads[:, :], qk[:, c, :], start=True, stop=False)
                        pe.wait_ge(s_qk2, 2 * KD * n + QK_ORDER.index(c) + 1)
                        nc.tensor.matmul(ps[:, 4 + c, :], minus_half_head[:, :], qk2[:, c, :],
                                         start=False, stop=True).then_inc(s_fps, 1)
                if r == NBAT:
                    keep_warm(7, WARM_TAIL[2])
                if late:
                    if early:
                        pe.wait_ge(s_f, 2 * KD * n + KD)
                    rows_T(NBAT + b, h, NBAT + rb)
                if early:
                    pe.wait_ge(s_f, 2 * KD * (n + 1))
                    for j in range(NJ):
                        for m in range(KD):
                            mm = nc.tensor.transpose(tok_banks(6)[:, j, m * P:(m + 1) * P],
                                                     kf[:, m, j * P:(j + 1) * P], ident[:, :])
                    mm.then_inc(s_ktps, 1)

            pe.wait_ge(s_const, N_CONST + 4)
            pe.wait_ge(s_rload, 16 * (P // HEAD_DIM))
            pe.wait_ge(s_scatter_go, NBAT + NS * E)
            keep_warm(7, WARM_X1[0])
            steps(pe, 0, 3, NBAT - 1, NBAT + 2, attend)
            pe.wait_ge(s_scatter_go, NBAT + NS * E + NBAT)
            keep_warm(5, WARM_ROUTED[1])
            slots_T(E, E // 2, E)
            keep_warm(5, WARM_SLOTS)
            steps(pe, E, E, 2 * E - 2, 2 * E, expert)

        @block.vector
        def _(dve):
            dve.memset(r_heads[:, :], 0.0).then_inc(s_rzero, 1)
            dve.memset(r_seen[0][:, 0, :], 0.0).then_inc(s_zero, 1)
            dve.wait_ge(s_const, N_CONST + 1)
            nc.vector.tensor_copy(rows_first[:, :, :, ID].rearrange("p n j -> p n j"),
                                  ids[:, :].rearrange("p (n j) -> p n j", j=NJ)).then_inc(s_rid_first, 1)

            def route_stats(n, h, r):
                x_at = route_rows(r)
                if r < NBAT:
                    dve.wait_ge(s_rx[r], 16)
                for j in range(NJ):
                    if r >= NBAT:
                        dve.wait_ge(s_x2, 2 * (n - NBAT) + j // 2 + 1)
                    ins = nc.vector.bn_stats(r_st[r % 2][:, j, :], x_at[:, j, 0:D])
                ins.then_inc(s_rst, 1)
                if r >= NBAT:
                    nc.vector.tensor_copy(x_at[:, :, ID:ID + 1],
                                          ids[:, bass.ds((n - NBAT) * NJ, NJ)][:, :, None]).then_inc(s_rid, 1)
                dve.wait_ge(s_rst, n + 1)
                if r > NBAT:
                    dve.wait_ge(s_rrs, n)
                dve.sem_inc(s_aggr_go, 1)
                for j in range(NJ):
                    ins = nc.vector.bn_aggr(route_mv(r)[:, j, :], r_st[r % 2][:, j, :])
                ins.then_inc(s_rvar, 1)

            def route_low(n, h, r):
                hi, lo = route_xT(r)
                for k in range(KD):
                    dve.wait_ge(s_rxhi, KD * n + k + 1)
                    nc.vector.tensor_tensor(lo[:, k, :], ps[:, route_bank(r) + k, :], hi[:, k, :],
                                            ALU.subtract).then_inc(s_rxlo, 1)

            def route_shift(n, h, r):
                x_at = route_rows(r)
                dve.wait_ge(s_rrs, n + 1)
                nc.vector.scalar_tensor_tensor(out=x_at[:, :, SHIFT:SHIFT + 1], in0=route_mv(r)[:, :, 0:1],
                                               scalar=-1.0, in1=x_at[:, :, RSTD:RSTD + 1],
                                               op0=ALU.mult, op1=ALU.mult).then_inc(s_rsh, 1)

            def route_choose(n, h, r):
                lg = ps[:, LOGITS[r // NBAT], 0:NJ * E].rearrange("p (j e) -> p j e", e=E)
                wide = [P, NJ, E]
                oh, seen, nxt, best = r_oh[r % 2], r_seen[r % 2], r_seen[1 - r % 2], r_best[r % 2]
                dve.wait_ge(s_rlg, n + 1)
                nc.vector.tensor_reduce(r_top[:, :], lg, AX.X, ALU.max).then_inc(s_rtop, 1)
                dve.wait_ge(s_rtop, n + 1)
                nc.vector.tensor_tensor(r_eq[:, :, :], lg, r_top[:, :, None].to_broadcast(wide),
                                        ALU.is_ge).then_inc(s_req, 1)
                if r >= 1:
                    dve.wait_ge(s_rex, n)
                nc.vector.tensor_tensor(r_dl[:, :, :], lg, r_top[:, :, None].to_broadcast(wide),
                                        ALU.subtract).then_inc(s_rdl, 1)
                dve.wait_ge(s_req, n + 1)
                nc.vector.tensor_tensor(r_sc[:, :, :], r_eq[:, :, :], rank[:, None, :].to_broadcast(wide),
                                        ALU.mult).then_inc(s_rsc, 1)
                dve.wait_ge(s_rsc, n + 1)
                nc.vector.tensor_reduce(best[:, :], r_sc[:, :, :], AX.X, ALU.max).then_inc(s_rbest, 1)
                dve.wait_ge(s_rbest, n + 1)
                if r >= 2:
                    dve.wait_ge(s_rcnt, n - 1)
                nc.vector.tensor_tensor(oh[:, :, :], r_sc[:, :, :], best[:, :, None].to_broadcast(wide),
                                        ALU.is_equal).then_inc(s_roh, 1)

            def route_seen(n, h, r):
                oh, seen, nxt = r_oh[r % 2], r_seen[r % 2], r_seen[1 - r % 2]
                if r % NBAT == NBAT - 1:
                    return
                dve.wait_ge(s_roh, n + 1)
                with nc.allow_low_precision(reason="counts up to 4, exact in bfloat16"):
                    nc.vector.tensor_reduce(r_sumj[:, :], oh[:, :, :].rearrange("p j e -> p e j"), AX.X,
                                            ALU.add).then_inc(s_rsumj, 1)
                skipped = r // NBAT
                dve.wait_ge(s_rsumj, n + 1 - skipped)
                if r >= 1:
                    dve.wait_ge(s_rcnt, n)
                if r % NBAT == 0:
                    dve.wait_ge(s_zero, r // NBAT + 1)
                nc.vector.tensor_tensor(nxt[:, 0, :], seen[:, 0, :], r_sumj[:, :], ALU.add).then_inc(s_rseen, 1)

            def route_place(n, h, r):
                x_at = route_rows(r)
                dve.wait_ge(s_rex, n + 1)
                nc.vector.tensor_reduce(r_sum[:, :], r_ex[:, :, :], AX.X, ALU.add).then_inc(s_rsum, 1)
                dve.wait_ge(s_rsum, n + 1)
                nc.vector.reciprocal(r_inv[:, :], r_sum[:, :]).then_inc(s_rinv, 1)
                dve.wait_ge(s_rcnt, n + 1)
                nc.vector.tensor_tensor(r_pm[:, :, :], r_oh[r % 2][:, :, :],
                                        ps[:, COUNTS[r // NBAT], 0:NJ * E].rearrange("p (j e) -> p j e", e=E),
                                        ALU.mult).then_inc(s_rpm, 1)
                dve.wait_ge(s_rinv, n + 1)
                nc.vector.tensor_scalar(x_at[:, :, GT:GT + 1], r_inv[:, :, None], 0.5, None,
                                        ALU.mult).then_inc(s_rgate, 1)
                dve.wait_ge(s_rpm, n + 1)
                nc.vector.tensor_reduce(r_pos[:, :], r_pm[:, :, :], AX.X, ALU.add).then_inc(s_rpos, 1)
                dve.wait_ge(s_rpos, n + 1)
                nc.vector.scalar_tensor_tensor(out=r_slot[:, :], in0=r_best[r % 2][:, :], scalar=-float(CAP),
                                               in1=r_pos[:, :], op0=ALU.mult, op1=ALU.add).then_inc(s_rslot, 1)
                nc.vector.tensor_scalar(r_over[:, :], r_pos[:, :], float(CAP), FAR, ALU.is_gt,
                                        ALU.mult).then_inc(s_rover, 1)
                dve.wait_ge(s_rslot, n + 1)
                dve.wait_ge(s_rover, n + 1)
                nc.vector.scalar_tensor_tensor(out=route_idx(r)[:, :], in0=r_slot[:, :], scalar=float(SLOTS - 1),
                                               in1=r_over[:, :], op0=ALU.add, op1=ALU.add).then_inc(s_ridx, 1)

            def projections_low():
                for i in range(4):
                    dve.wait_ge(s_wT, i + 1)
                    nc.vector.scalar_tensor_tensor(out=wT_lo[:, i, :, :].rearrange("p k d -> p (k d)"),
                                                   in0=ps[:, i, :], scalar=W_SCALE,
                                                   in1=wT_hi[:, i, :, :].rearrange("p k d -> p (k d)"),
                                                   op0=ALU.mult, op1=ALU.subtract).then_inc(s_wTlo, 1)
                dve.wait_ge(s_wg, 16)
                nc.vector.tensor_scalar(wg_hi[:, :, :], wg_sb[:, :, :], W_SCALE, None, ALU.mult).then_inc(s_wghi, 1)
                dve.wait_ge(s_wghi, 1)
                nc.vector.scalar_tensor_tensor(out=wg_lo[:, :, :], in0=wg_sb[:, :, :], scalar=W_SCALE,
                                               in1=wg_hi[:, :, :], op0=ALU.mult, op1=ALU.subtract).then_inc(s_wglo, 1)

            for n in range(NBAT + 1):
                if n == 2:
                    projections_low()
                if n < NBAT:
                    route_stats(n, n // 2, n)
                if n >= 1:
                    route_shift(n - 1, (n - 1) // 2, n - 1)
            route_low(0, 0, 0)
            for n in range(NBAT + 1):
                if n + 1 < NBAT:
                    route_low(n + 1, (n + 1) // 2, n + 1)
                if n < NBAT:
                    route_choose(n, n // 2, n)
                    route_seen(n, n // 2, n)
                if n >= 1:
                    route_place(n - 1, (n - 1) // 2, n - 1)

            def slots_norm(n, h, r):
                at = xe[r % 2]
                ph = r // E
                if r % E:
                    dve.wait_ge(s_xe[r % 2], 16 * (h + 1 if r % 2 else h - ph))
                if r >= 1:
                    dve.wait_ge(s_xtp, 3 * n)
                for s in range(NS):
                    for i, (lo, hi) in enumerate(SLOT_PIECES):
                        if r % E == 0 and s == lo:
                            dve.wait_ge(s_xe_first[i], 16 * (ph + 1))
                    nc.vector.tensor_scalar(xs[:, s, :], at[:, s, 0:D], at[:, s, RSTD:RSTD + 1],
                                            at[:, s, SHIFT:SHIFT + 1], ALU.mult, ALU.add).then_inc(s_xs, 1)
                if r >= 2:
                    dve.wait_ge(s_yscat[r % 2], 16 * NS * h)
                nc.vector.tensor_copy(y_idx[r % 2][:, :, None], at[:, :, ID:ID + 1]).then_inc(s_yid, 1)

            def w1_low(n, h, r, k):
                dve.wait_ge(s_w1hi, KD * n + k + 1)
                nc.vector.scalar_tensor_tensor(out=w1_lo[:, k, :], in0=w1_sb[r % 2][:, k, :], scalar=W_SCALE,
                                               in1=w1_hi[:, k, :], op0=ALU.mult,
                                               op1=ALU.subtract).then_inc(s_w1lo, 1)

            def w2_low(n, h, r, i):
                at = slice(i * FM // 2, (i + 1) * FM // 2)
                dve.wait_ge(s_w2hi, 2 * n + i + 1)
                nc.vector.scalar_tensor_tensor(out=w2_lo[:, at, :], in0=w2_sb[r % 2][:, at, :], scalar=W_SCALE,
                                               in1=w2_hi[:, at, :], op0=ALU.mult,
                                               op1=ALU.subtract).then_inc(s_w2lo, 1)

            def slots_T_low(n, h, r):
                for c in range((NS + 1) // 2):
                    w = min(2, NS - 2 * c) * P
                    dve.wait_ge(s_xhi, 3 * n + c + 1)
                    nc.vector.tensor_tensor(xT_lo[:, :, 2 * c * P:2 * c * P + w],
                                            ps[:, T_BANKS[c], :].rearrange("p (k t) -> p k t", k=KD)[:, :, 0:w],
                                            xT_hi[:, :, 2 * c * P:2 * c * P + w], ALU.subtract).then_inc(s_xlo, 1)

            def h_low(n, h, r, m):
                dve.wait_ge(s_hf, FM * n + m + 1)
                nc.vector.tensor_tensor(hT_lo[:, m, :], h_full[:, m % 2, :], hT_hi[:, m, :],
                                        ALU.subtract).then_inc(s_hlo, 1)

            def slot_add(n, h, r, s):
                at = xe[r % 2]
                q = s % 2 if r % 2 == 0 else (s + 1) % 2
                dve.wait_ge(s_y, NS * n + s + 1)
                if r >= 1 or s >= 2:
                    dve.wait_ge(s_yrow, NS * n + s - 1)
                nc.vector.scalar_tensor_tensor(out=y_b[:, q, :], in0=ps[:, 4 + q, 0:D],
                                               scalar=1.0 / (H_SCALE * W_SCALE),
                                               in1=b2_sb[:, bass.ds(n - (r // E) * E, 1), :].rearrange(
                                                   "p e d -> p (e d)"),
                                               op0=ALU.mult, op1=ALU.add).then_inc(s_yb, 1)
                dve.wait_ge(s_yb, NS * n + s + 1)
                nc.vector.scalar_tensor_tensor(out=y_rows[r % 2][:, s, :], in0=y_b[:, q, :],
                                               scalar=at[:, s, GT:GT + 1], in1=at[:, s, 0:D],
                                               op0=ALU.mult, op1=ALU.add).then_inc(s_yrow, 1)

            def expert(n, h, r):
                hn = h if r % 2 == 0 else h + 1
                for m in range(FM):
                    h_low(n, h, r, m)
                    if m in (FM // 2 - 1, FM // 2 + 1):
                        w2_low(n, h, r, (m - FM // 2 + 1) // 2)
                    if m == FM // 2 and r % E != E - 1:
                        slots_norm(n + 1, hn, r + 1)
                if r % E != E - 1:
                    slots_T_low(n + 1, hn, r + 1)
                for s in range(NS):
                    slot_add(n, h, r, s)
                    if s in (1, 3) and r % E != E - 1:
                        w1_low(n + 1, hn, r + 1, s // 2)

            dve.wait_ge(s_bload, 48)
            for k in range(KD):
                w1_low(0, 0, 0, k)
            slots_norm(0, 0, 0)
            slots_T_low(0, 0, 0)
            steps(dve, 0, 2, E - 2, E, expert)

            def norm_stats(n, h, r):
                if r >= 1:
                    dve.wait_ge(s_ax[r % 2], 16 * (h + r % 2))
                for j in range(NJ):
                    if r == 0 and j % (NJ // 2) == 0:
                        dve.wait_ge(s_ax_first[j // (NJ // 2)], 16)
                    ins = nc.vector.bn_stats(a_st[:, j, :], x1[r % 2][:, j, :])
                ins.then_inc(s_ast, 1)
                dve.wait_ge(s_ast, n + 1)
                dve.sem_inc(s_aggr_go, 1)
                for j in range(NJ):
                    ins = nc.vector.bn_aggr(a_mv[:, j, :], a_st[:, j, :])
                ins.then_inc(s_avar, 1)

            def norm_shift(n, h, r):
                dve.wait_ge(s_ars, n + 1)
                if r >= 1:
                    dve.wait_ge(s_axn, NJ * n)
                nc.vector.scalar_tensor_tensor(out=a_rs[:, :, 0:1], in0=a_mv[:, :, 0:1], scalar=-1.0,
                                               in1=a_rs[:, :, 1:2], op0=ALU.mult, op1=ALU.mult).then_inc(s_ash, 1)

            def attend(n, h, r):
                early, late, placed = r < NBAT, 1 <= r <= NBAT, r >= 2
                b, rb = n - 1, r - 1
                hb = h - 1 if r % 2 == 0 else h
                hn = h if r % 2 == 0 else h + 1
                if r < NBAT - 1:
                    norm_stats(n + 1, hn, r + 1)
                if late:
                    dve.wait_ge(s_kvps, b + 1)
                    if rb >= 1:
                        dve.wait_ge(s_ops, b)
                    nc.vector.tensor_tensor(kv[:, :, 0:P], ps[:, 2, 0:D].rearrange("p (m e) -> p m e", e=P),
                                            same_head[:, None, :].to_broadcast([P, KD, P]),
                                            ALU.mult).then_inc(s_kv, 1)
                if early:
                    for k in range(KD):
                        dve.wait_ge(s_axhi, KD * n + k + 1)
                        nc.vector.tensor_tensor(a_xT_lo[:, k, :], ps[:, k, :], a_xT_hi[:, k, :],
                                                ALU.subtract).then_inc(s_axlo, 1)
                if placed:
                    route_choose(NBAT + n - 2, h, NBAT + r - 2)
                    route_seen(NBAT + n - 2, h, NBAT + r - 2)
                if late:
                    def out_blocks(bank, blocks):
                        return ps[:, bank, 0:blocks * (P + NH)].rearrange("p (g c) -> p g c", c=P + NH)

                    dve.wait_ge(s_ops, b + 1)
                    for bank, first, blocks in OUT_BANKS:
                        nc.vector.tensor_scalar(zt[:, first:first + blocks, :], out_blocks(bank, blocks)[:, :, P:P + NH],
                                                EPS_Z, None, ALU.add).then_inc(s_zt, 1)
                    dve.wait_ge(s_zt, len(OUT_BANKS) * (b + 1))
                    nc.vector.reciprocal(zr[:, :, :], zt[:, :, :]).then_inc(s_z, 1)
                    dve.wait_ge(s_z, b + 1)
                    if rb >= 1:
                        dve.wait_ge(s_otp, b)
                    for bank, first, blocks in OUT_BANKS:
                        ins = nc.vector.tensor_tensor(
                            o_tok[:, first * P:(first + blocks) * P].rearrange("p (g a e) -> p g a e", g=blocks,
                                                                               e=HEAD_DIM),
                            out_blocks(bank, blocks)[:, :, 0:P].rearrange("p g (a e) -> p g a e", e=HEAD_DIM),
                            zr[:, first:first + blocks, :, None].to_broadcast([P, blocks, NH, HEAD_DIM]), ALU.mult)
                    ins.then_inc(s_o, 1)
                if placed:
                    route_place(NBAT + n - 2, h, NBAT + r - 2)
                if early:
                    for i, c in enumerate(QK_ORDER):
                        dve.wait_ge(s_qkps, 2 * KD * n + i + 1)
                        if i == 0 and r >= 1:
                            dve.wait_ge(s_fps, 2 * KD * n)
                        nc.vector.tensor_scalar(qk[:, c, :], ps[:, 4 + c, :], QSCALE / W_SCALE, qk_bias[:, c:c + 1],
                                                ALU.mult, ALU.add).then_inc(s_qk, 1)
                if late:
                    for k in range(KD):
                        dve.wait_ge(s_ohi, KD * b + k + 1)
                        nc.vector.tensor_tensor(oT_lo[:, k, :], ps[:, k, :], oT_hi[:, k, :],
                                                ALU.subtract).then_inc(s_olo, 1)
                if early:
                    dve.wait_ge(s_vps, n + 1)
                    if r >= 2:
                        dve.wait_ge(s_kvps, n - 1)
                    nc.vector.scalar_tensor_tensor(out=vt[r % 2][:, :, :], in0=tok_banks(2), scalar=1.0 / W_SCALE,
                                                   in1=bv_sb[:, :, :].to_broadcast([P, NJ, D]),
                                                   op0=ALU.mult, op1=ALU.add).then_inc(s_v, 1)
                if r < NBAT - 1:
                    norm_shift(n + 1, hn, r + 1)
                if late:
                    dve.wait_ge(s_xb, b + 1)
                    if rb >= 2:
                        dve.wait_ge(s_rscat[rb % 2], 16 * NJ * hb)
                        dve.wait_ge(s_keep[rb % 2], 16 * hb)
                    for i in range(2):
                        at = slice(2 * i, 2 * i + 2)
                        dve.wait_ge(s_yps, 2 * b + i + 1)
                        nc.vector.scalar_tensor_tensor(out=rows[rb % 2][:, at, 0:D], in0=tok_banks(0)[:, at, :],
                                                       scalar=1.0 / W_SCALE, in1=xb[rb % 2][:, at, :],
                                                       op0=ALU.mult, op1=ALU.add).then_inc(s_x2, 1)
                    route_stats(NBAT + b, NBAT // 2 + hb, NBAT + rb)
                    route_shift(NBAT + b, NBAT // 2 + hb, NBAT + rb)
                    route_low(NBAT + b, NBAT // 2 + hb, NBAT + rb)

            dve.wait_ge(s_const, N_CONST + 4)
            dve.wait_ge(s_wT, 6)
            dve.wait_ge(s_rcnt, NBAT)
            nc.vector.memset(r_seen[0][:, 0, :], 0.0).then_inc(s_zero, 1)
            norm_stats(0, 0, 0)
            norm_shift(0, 0, 0)
            steps(dve, 0, 3, NBAT - 1, NBAT + 2, attend)
            for k in range(KD):
                w1_low(E, E // 2, E, k)
            slots_norm(E, E // 2, E)
            slots_T_low(E, E // 2, E)
            steps(dve, E, E, 2 * E - 2, 2 * E, expert)


_INS = ["L0_attn_x", "L0_attn_Wq", "L0_attn_bq", "L0_attn_Wk", "L0_attn_bk", "L0_attn_Wv", "L0_attn_bv",
        "L0_attn_Wo", "L0_attn_bo", "L0_attn_R", "L0_ffn_wg", "L0_ffn_w1", "L0_ffn_b1", "L0_ffn_w2", "L0_ffn_b2"]
_OUTS = [((8, 512, 256), "float32")]


def kernel(**inputs):
    import numpy as _np
    import concourse.bacc as _bacc
    from concourse import mybir as _mybir
    from concourse.bass_utils import run_bass_kernel_spmd as _run

    nc = _bacc.Bacc("TRN2", target_bir_lowering=False, num_devices=1)
    arrays, args = {}, []
    for name in _INS:
        a = _np.ascontiguousarray(inputs[name])
        arrays[f"in_{name}_dram"] = a
        args.append(nc.dram_tensor(f"in_{name}_dram", a.shape, _mybir.dt.from_np(a.dtype), kind="ExternalInput").ap())
    for i, (shape, dtype) in enumerate(_OUTS):
        dt = _mybir.dt.from_np(_np.dtype(dtype))
        args.append(nc.dram_tensor(f"out_{i}_dram", shape, dt, kind="ExternalOutput").ap())
    macaron_kernel(nc, *args)
    r = _run(nc, [arrays], core_ids=[0])
    got = tuple(r.results[0][f"out_{i}_dram"] for i in range(len(_OUTS)))
    return got[0]
```
